# Optimizing a Trainium2 kernel written in Bass

```python
import numpy as np
import jax
import jax.numpy as jnp

def _softmax(x, axis=-1):
    return jax.nn.softmax(x, axis=axis)

def _gelu(x):
    return jax.nn.gelu(x, approximate=True)

def _silu(x):
    return jax.nn.silu(x)

def _sigmoid(x):
    return jax.nn.sigmoid(x)

def _layernorm(x, axis=-1, eps=1e-05):
    m = jnp.mean(x, axis=axis, keepdims=True)
    v = jnp.var(x, axis=axis, keepdims=True)
    return (x - m) / jnp.sqrt(v + eps)

def _scatter_add(tgt, idx, src, axis=0):
    return tgt.at[idx].add(src)

def _segment_sum(src, seg, n):
    return jax.ops.segment_sum(src, seg, n)
kernel_name = 'mk_vit_tower_d1_tok_img1024_r4_af52ec'

def setup_inputs(seed: int=0):
    np.random.seed(seed)
    _w = jnp.asarray

    def _rec_inputs():
        import jax
        import jax.numpy as jnp
        _rk = jax.random.key(seed)
        x = -0.00016672 + 0.999947 * jax.random.normal(jax.random.fold_in(_rk, 1), (16, 3, 96, 96), jnp.float32)
        return x
    x = _rec_inputs()

    def _L0_tok_setup():
        import jax, jax.numpy as jnp
        import numpy as np
        IMG = 96
        PATCH = 16
        C_IN = 3
        EMBED = 256
        NPH = IMG // PATCH
        NUM_PATCHES = NPH * NPH
        PATCH_DIM = PATCH * PATCH * C_IN
        key = jax.random.key(seed)
        k_x, k_w, k_b, k_cls, k_pos = jax.random.split(key, 5)
        x = jax.random.normal(k_x, (64, C_IN, IMG, IMG), dtype=jnp.float32)
        W = jax.random.normal(k_w, (EMBED, PATCH_DIM), dtype=jnp.float32) * (1.0 / np.sqrt(PATCH_DIM))
        b = jax.random.normal(k_b, (EMBED,), dtype=jnp.float32) * 0.01
        cls_token = jax.random.normal(k_cls, (1, 1, EMBED), dtype=jnp.float32) * 0.02
        pos_embed = jax.random.normal(k_pos, (1, NUM_PATCHES + 1, EMBED), dtype=jnp.float32) * 0.02
        return {'x': x, 'W': W, 'b': b, 'cls_token': cls_token, 'pos_embed': pos_embed}
    _L0_tok_all = _L0_tok_setup()
    _L0_tok_in = {k: v for k, v in _L0_tok_all.items() if k in ('W', 'b', 'cls_token', 'pos_embed')}
    del _L0_tok_all

    def _L0_attn_setup():
        import jax, jax.numpy as jnp
        import numpy as np
        B, S, D = (2, 512, 256)
        H, DH = (16, 64)
        N_CTX = 512
        IGNORE = -100000.0
        key = jax.random.key(seed)
        ks = jax.random.split(key, 6)
        scale = 0.02
        return {'x': jax.random.normal(ks[0], (B, S, D), dtype=jnp.float32), 'W_Q': jax.random.normal(ks[1], (H, DH, D), dtype=jnp.float32) * scale, 'W_K': jax.random.normal(ks[2], (H, DH, D), dtype=jnp.float32) * scale, 'W_V': jax.random.normal(ks[3], (H, DH, D), dtype=jnp.float32) * scale, 'W_O': jax.random.normal(ks[4], (H, D, DH), dtype=jnp.float32) * scale, 'b_Q': jnp.zeros((H, DH), dtype=jnp.float32), 'b_K': jnp.zeros((H, DH), dtype=jnp.float32), 'b_V': jnp.zeros((H, DH), dtype=jnp.float32), 'b_O': jnp.zeros((D,), dtype=jnp.float32)}
    _L0_attn_all = _L0_attn_setup()
    _L0_attn_in = {k: v for k, v in _L0_attn_all.items() if k in ('W_Q', 'W_K', 'W_V', 'W_O', 'b_Q', 'b_K', 'b_V', 'b_O')}
    del _L0_attn_all

    def _L0_ffn_setup():
        import jax, jax.numpy as jnp
        import numpy as np
        EPS = 1e-05

        def _quantize(W):
            gamma = jnp.mean(jnp.abs(W))
            return jnp.clip(jnp.round(W / (gamma + EPS)), -1.0, 1.0)
        key = jax.random.key(seed)
        k_x, k_w1, k_b1, k_w2, k_b2 = jax.random.split(key, 5)
        n_embd = 256
        d_ff = 4 * n_embd
        B, S = (4, 1024)
        bound1 = 1.0 / np.sqrt(n_embd)
        bound2 = 1.0 / np.sqrt(d_ff)
        x = jax.random.normal(k_x, (B, S, n_embd), dtype=jnp.float32)
        W1 = jax.random.uniform(k_w1, (d_ff, n_embd), jnp.float32, -bound1, bound1)
        b1 = jax.random.uniform(k_b1, (d_ff,), jnp.float32, -bound1, bound1)
        W2 = jax.random.uniform(k_w2, (n_embd, d_ff), jnp.float32, -bound2, bound2)
        b2 = jax.random.uniform(k_b2, (n_embd,), jnp.float32, -bound2, bound2)
        return {'x': x, 'W1': W1, 'b1': b1, 'W2': W2, 'b2': b2}
    _L0_ffn_all = _L0_ffn_setup()
    _L0_ffn_in = {k: v for k, v in _L0_ffn_all.items() if k in ('W1', 'b1', 'W2', 'b2')}
    del _L0_ffn_all
    return {'x': x, 'L0_tok_W': _L0_tok_in['W'], 'L0_tok_b': _L0_tok_in['b'], 'L0_tok_cls_token': _L0_tok_in['cls_token'], 'L0_tok_pos_embed': _L0_tok_in['pos_embed'], 'L0_attn_W_Q': _L0_attn_in['W_Q'], 'L0_attn_W_K': _L0_attn_in['W_K'], 'L0_attn_W_V': _L0_attn_in['W_V'], 'L0_attn_W_O': _L0_attn_in['W_O'], 'L0_attn_b_Q': _L0_attn_in['b_Q'], 'L0_attn_b_K': _L0_attn_in['b_K'], 'L0_attn_b_V': _L0_attn_in['b_V'], 'L0_attn_b_O': _L0_attn_in['b_O'], 'L0_ffn_W1': _L0_ffn_in['W1'], 'L0_ffn_b1': _L0_ffn_in['b1'], 'L0_ffn_W2': _L0_ffn_in['W2'], 'L0_ffn_b2': _L0_ffn_in['b2']}

def reference(x, L0_tok_W, L0_tok_b, L0_tok_cls_token, L0_tok_pos_embed, L0_attn_W_Q, L0_attn_W_K, L0_attn_W_V, L0_attn_W_O, L0_attn_b_Q, L0_attn_b_K, L0_attn_b_V, L0_attn_b_O, L0_ffn_W1, L0_ffn_b1, L0_ffn_W2, L0_ffn_b2):
    import jax
    import jax.numpy as jnp

    def _L0_tok_ref(x, W, b, cls_token, pos_embed):
        import jax, jax.numpy as jnp
        import numpy as np
        IMG = 96
        PATCH = 16
        C_IN = 3
        EMBED = 256
        NPH = IMG // PATCH
        NUM_PATCHES = NPH * NPH
        PATCH_DIM = PATCH * PATCH * C_IN
        B, C, H, Wd = x.shape
        nph, npw = (H // PATCH, Wd // PATCH)
        patches = x.reshape(B, C, nph, PATCH, npw, PATCH)
        patches = patches.transpose(0, 2, 4, 1, 3, 5)
        patches = patches.reshape(B, nph * npw, C * PATCH * PATCH)
        proj = jnp.einsum('bnd,ed->bne', patches, W) + b
        cls = jnp.broadcast_to(cls_token, (B, 1, cls_token.shape[-1]))
        out = jnp.concatenate([cls, proj], axis=1) + pos_embed
        return out

    def _L0_attn_ref(x, W_Q, W_K, W_V, W_O, b_Q, b_K, b_V, b_O):
        import jax, jax.numpy as jnp
        import numpy as np
        B, S, D = (2, 512, 256)
        H, DH = (16, 64)
        N_CTX = 512
        IGNORE = -100000.0
        attn_scale = jnp.sqrt(jnp.asarray(DH, dtype=x.dtype))
        q = jnp.einsum('ihm,bpm->bpih', W_Q, x) + b_Q
        k = jnp.einsum('ihm,bpm->bpih', W_K, x) + b_K
        v = jnp.einsum('ihm,bpm->bpih', W_V, x) + b_V
        attn_scores = jnp.einsum('bpih,bqih->bipq', q, k) / attn_scale
        qs, ks_ = (attn_scores.shape[-2], attn_scores.shape[-1])
        mask = jnp.tril(jnp.ones((qs, ks_), dtype=bool))
        attn_scores = jnp.where(mask, attn_scores, jnp.asarray(IGNORE, dtype=attn_scores.dtype))
        attn_matrix = jax.nn.softmax(attn_scores, axis=-1)
        z = jnp.einsum('bpih,biqp->bqih', v, attn_matrix)
        out = jnp.einsum('idh,bqih->bqd', W_O, z) + b_O
        return out

    def _L0_ffn_ref(x, W1, b1, W2, b2):
        import jax, jax.numpy as jnp
        import numpy as np
        EPS = 1e-05

        def _quantize(W):
            gamma = jnp.mean(jnp.abs(W))
            return jnp.clip(jnp.round(W / (gamma + EPS)), -1.0, 1.0)
        Wq1 = _quantize(W1)
        Wq2 = _quantize(W2)
        h = jax.nn.relu(jnp.einsum('bsd,fd->bsf', x, Wq1) + b1)
        out = jnp.einsum('bsf,df->bsd', h, Wq2) + b2
        return out
    h = _L0_tok_ref(x, L0_tok_W, L0_tok_b, L0_tok_cls_token, L0_tok_pos_embed)
    h = h + _L0_attn_ref(_layernorm(h, axis=-1), L0_attn_W_Q, L0_attn_W_K, L0_attn_W_V, L0_attn_W_O, L0_attn_b_Q, L0_attn_b_K, L0_attn_b_V, L0_attn_b_O)
    h = h + _L0_ffn_ref(_layernorm(h, axis=-1), L0_ffn_W1, L0_ffn_b1, L0_ffn_W2, L0_ffn_b2)
    return h

_drawn_inputs = setup_inputs


def setup_inputs(seed=0):
    import zlib

    import numpy as np

    out = dict(_drawn_inputs(seed))
    spreads = {'L0_attn_b_Q': (0.0, 0.8),
     'L0_attn_b_K': (0.0, 2.0),
     'L0_attn_b_V': (0.0, 0.1),
     'L0_attn_b_O': (0.0, 0.1)}
    factors = {'L0_tok_b': 5.327,
     'L0_attn_W_Q': 8.0,
     'L0_attn_W_K': 8.0,
     'L0_ffn_b1': 21.545,
     'L0_ffn_b2': 64.0}
    for name, (base, spread) in spreads.items():
        noise = np.random.default_rng([zlib.crc32(name.encode()), seed]).standard_normal(out[name].shape)
        drawn = base * np.exp(spread * noise) if base else spread * noise
        out[name] = jnp.asarray(drawn.astype(out[name].dtype))
    for name, factor in factors.items():
        out[name] = (out[name] * factor).astype(out[name].dtype)
    return out
```

```python
import concourse.bass as bass
from concourse import mybir
from contextlib import ExitStack

F32 = mybir.dt.float32
F32R = mybir.dt.float32r
ALU = mybir.AluOpType
ACT = mybir.ActivationFunctionType
AX = mybir.AxisListType

IMAGES, SEQ, DIM = 16, 37, 256
TOKENS = IMAGES * SEQ
PATCH_DIM = 3 * 16 * 16
KP = PATCH_DIM // 128
KD = DIM // 128
HEADS, HEAD_DIM = 16, 64
PAIRS = HEADS // 2
FF = 1024
FT = FF // 128
TILES = [(t, min(128, TOKENS - t)) for t in range(0, TOKENS, 128)]
NT = len(TILES)
PER_GROUP = 128 // SEQ
GROUP = PER_GROUP * SEQ
GROUPS = [(g, min(GROUP, TOKENS - g)) for g in range(0, TOKENS, GROUP)]
NG = len(GROUPS)
UNITS = 2 * NG
UW = GROUP + 1
HALF = TOKENS // 2
ZHALF = [(0, 3 * GROUP), (3 * GROUP, TOKENS)]
FFN_CHUNKS = [(0, 256, 0, 2), (256, TOKENS, 2, NT)]
EPS = 1e-5
SCALE = float(HEAD_DIM) ** -0.5
HIDDEN_KEY = -1e5 / SCALE
OTHER_IMAGE = -1e30


def vit_block(nc, xw, wqk, wv, wo, w1, w2, bias_cols, bias_rows, tok_bias, cls, pos, out):
    with ExitStack() as ctx:
        def sb(name, shape, dt=F32):
            return ctx.enter_context(nc.sbuf_tensor(name, shape, dt))

        def early(name, shape, dt, heir, heir_shape, heir_dt):
            with nc.sbuf_tensor(heir, heir_shape, heir_dt) as late:
                pass
            return sb(name, shape, dt), late

        def sem(name):
            return ctx.enter_context(nc.semaphore(name))

        xw_sb, h_hi = early("xw_sb", [128, KP, TOKENS + DIM], F32, "h_hi", [128, FT, TOKENS], F32R)
        wqk_sb = sb("wqk_sb", [128, PAIRS * KD * 256])
        wv_sb = sb("wv_sb", [128, KD, FF])
        wo_sb = sb("wo_sb", [128, PAIRS, DIM])
        w1_sb, hr2 = early("w1_sb", [128, KD * FF], F32, "hr", [128, 2, TOKENS], F32)
        w2_sb, y = early("w2_sb", [128, FT * DIM], F32, "y", [128, NT, DIM], F32)
        hr = [hr2[:, n, :] for n in range(2)]
        cols = sb("cols", [128, 4 * 8])
        rows = sb("rows", [128, 2 * DIM])
        pos_sb = sb("pos_sb", [SEQ, DIM])
        first_sb = sb("first_sb", [SEQ, DIM])
        ident = sb("ident", [128, 128])
        onehot = sb("onehot", [SEQ, TOKENS])
        mask = sb("mask", [GROUP, UW])
        ones = sb("ones", [128, 128])
        power = sb("power", [128, 1])
        wv_split, zT = early("wv_split", [128, 2 * KD + 1, FF], F32R, "zT", [128, PAIRS * TOKENS], F32)
        wv_hi, wv_lo = wv_split[:, 0:KD, :], wv_split[:, KD:2 * KD, :]
        wqk_hi = [sb(f"wqk_hi{n}", [128, KD * 256], F32R) for n in range(2)]
        wqk_lo = [sb(f"wqk_lo{n}", [128, KD * 256], F32R) for n in range(2)]
        w1q, w2q = sb("w1q", [128, KD * FF], F32R), sb("w2q", [128, FT * DIM], F32R)
        below = wv_sb[:, :, :].rearrange("p k n -> p (k n)")
        absum = sb("absum", [128, 2])
        gate = sb("gate", [128, 4])
        h0 = sb("h0", [128, NT, DIM])
        h1 = sb("h1", [128, NT, DIM])
        stat = sb("stat", [128, NT, 6])
        mv = sb("mv", [128, NT, 2])
        ve = sb("ve", [128, NT])
        rs0, rs1 = sb("rs0", [128, NT]), sb("rs1", [128, NT])
        rt0, rt1 = sb("rt0", [128, NT]), sb("rt1", [128, NT])
        xn = sb("xn", [128, NT, DIM])
        XC = GROUP * NG
        xn_hi, xn_lo = sb("xn_hi", [128, KD, XC], F32R), sb("xn_lo", [128, KD, XC], F32R)
        V, h_lo = early("V", [GROUP, NG, FF], F32, "h_lo", [128, FT, TOKENS], F32R)
        Vp = [sb(f"Vp{n}", [GROUP, NG, 128]) for n in range(2)]
        QT = [sb(f"QT{n}", [128, TOKENS]) for n in range(2)]
        KT = [sb(f"KT{n}", [128, TOKENS]) for n in range(2)]
        SM = sb("SM", [GROUP, UNITS, UW])
        nmax = sb("nmax", [GROUP, UNITS])
        rsum = sb("rsum", [GROUP, UNITS])
        rinv = sb("rinv", [GROUP, UNITS])
        P = [sb(f"P{n}", [GROUP, UNITS, UW]) for n in range(2)]
        PT = [sb(f"PT{n}", [GROUP, 2, UW]) for n in range(2)]

        B = [ctx.enter_context(nc.psum_tensor(f"bank{n}", [128, 512], F32)) for n in range(8)]
        S_BANK, T_BANK, Z_BANK, J_BANK = B[0:2], B[2:4], B[4:6], B[6:8]

        ld_xw = [sem(f"ld_xw{k}") for k in range(KP)]
        ld_small, ld_cols, ld_rows = sem("ld_small"), sem("ld_cols"), sem("ld_rows")
        ld_wqk, ld_wv, ld_wo, ld_w1, ld_w2 = (sem(f"ld_{n}") for n in ("wqk", "wv", "wo", "w1", "w2"))
        filled = sem("filled")
        consts_ready = sem("consts_ready")
        zeros_ready = sem("zeros_ready")
        add_ready = sem("add_ready")
        emb_done = sem("emb_done")
        h_ready = sem("h_ready")
        stat_done, mv_done, ve_ready = sem("stat_done"), sem("mv_done"), sem("ve_ready")
        pow_done, nt_a, nt_b, rstd_ready = sem("pow_done"), sem("nt_a"), sem("nt_b"), sem("rstd_ready")
        xn_done = sem("xn_done")
        xt_done = sem("xt_done")
        xh_done, xn_ready = sem("xh_done"), sem("xn_ready")
        wvh_done, wv_ready = sem("wvh_done"), sem("wv_ready")
        wqh_done, wq_ready = sem("wqh_done"), sem("wq_ready")
        abs_done, total_done, gam_done, gate_done, gate_ready = (
            sem(n) for n in ("abs_done", "total_done", "gam_done", "gate_done", "gate_ready"))
        below_done, wff_ready = sem("below_done"), sem("wff_ready")
        v_done = sem("v_done")
        va_ready, vd_ready = sem("va_ready"), sem("vd_ready")
        vp_ready = sem("vp_ready")
        proj_done = sem("proj_done")
        q_ready, k_ready = sem("q_ready"), sem("k_ready")
        s_done, sm_ready, exp_done = sem("s_done"), sem("sm_ready"), sem("exp_done")
        inv_ready, p_ready = sem("inv_ready"), sem("p_ready")
        t_done = sem("t_done")
        pt_ready = [sem("pt_even_ready"), sem("pt_odd_ready")]
        z_done, z_ready = [sem("z0_done"), sem("z1_done")], [sem("z0_ready"), sem("z1_ready")]
        hb0_ready, hb1_ready = sem("hb0_ready"), sem("hb1_ready")
        o_done = sem("o_done")
        f1_done, relu_done, hh_done, ff_ready = sem("f1_done"), sem("relu_done"), sem("hh_done"), sem("ff_ready")
        f2_done, y_ready, stored = sem("f2_done"), sem("y_ready"), sem("stored")

        block = ctx.enter_context(nc.Block())

        def cols_of(group_units, j):
            return cols[:, bass.ds(group_units * 8 + j, 1)]

        def steps(eng, step):
            step(0, 0)
            with eng.Fori(0, PAIRS // 2 - 1) as twice:
                step(twice * 2 + 1, 1)
                step(twice * 2 + 2, 0)
            step(PAIRS - 1, 1)
            step(PAIRS, 0)

        def count(eng, value):
            if not isinstance(value, int):
                eng.lower_val(value)
            return value

        def has(j, lo, hi):
            return lo <= j < hi if isinstance(j, int) else True

        @block.sync
        def _(sp):
            for k in range(KP):
                sp.dma_start(xw_sb[:, k, :], xw[k]).then_inc(ld_xw[k], 16)
            sp.dma_start(wv_sb[:, :, :], wv).then_inc(ld_wv, 16)
            sp.dma_start(wqk_sb[:, :], wqk).then_inc(ld_wqk, 16)
            sp.dma_start(w1_sb[:, :], w1).then_inc(ld_w1, 16)
            sp.dma_start(w2_sb[:, :], w2).then_inc(ld_w2, 16)
            sp.dma_start(wo_sb[:, :, :], wo).then_inc(ld_wo, 16)
            for i, (t, n) in enumerate(TILES):
                sp.wait_ge(y_ready, i + 1)
                sp.dma_start(out[t:t + n, :], y[0:n, i, :]).then_inc(stored, 16)
            sp.wait_ge(stored, 16 * NT)

        @block.gpsimd
        def _(pool):
            pool.memset(onehot[:, :], 0.0).then_inc(filled, 1)
            pool.memset(ident[:, :], 0.0).then_inc(filled, 1)
            pool.memset(mask[:, :], 0.0).then_inc(filled, 1)
            pool.memset(power[:, :], -0.5).then_inc(filled, 1)
            pool.wait_ge(filled, 4)
            pool.affine_select(out=onehot[:, :], in_=onehot[:, :], compare_op=ALU.not_equal, fill=1.0, base=0,
                               pattern=[[0, IMAGES], [-1, SEQ]], channel_multiplier=1).then_inc(consts_ready, 1)
            pool.affine_select(out=ident[:, :], in_=ident[:, :], compare_op=ALU.not_equal, fill=1.0, base=0,
                               pattern=[[-1, 128]], channel_multiplier=1).then_inc(consts_ready, 1)
            mk = mask[:, 0:GROUP]
            pool.affine_select(out=mk, in_=mk, compare_op=ALU.is_ge, fill=HIDDEN_KEY, base=0,
                               pattern=[[-1, GROUP]], channel_multiplier=1).then_inc(filled, 1)
            pool.wait_ge(filled, 5)
            pool.affine_select(out=mk, in_=mk, compare_op=ALU.is_ge, fill=OTHER_IMAGE, base=0,
                               pattern=[[-SEQ, PER_GROUP], [0, SEQ]], channel_multiplier=1).then_inc(filled, 1)
            pool.wait_ge(filled, 6)
            pool.affine_select(out=mk, in_=mk, compare_op=ALU.is_ge, fill=OTHER_IMAGE, base=SEQ - 1,
                               pattern=[[SEQ, PER_GROUP], [0, SEQ]], channel_multiplier=-1).then_inc(consts_ready, 1)

            def inverse_root(i, rs):
                pool.wait_ge(ve_ready, i + 1)
                t = i % NT
                n = TILES[t][1]
                pool.tensor_tensor(rs[0:n, t:t + 1], ve[0:n, t:t + 1], power[0:n, :], ALU.pow).then_inc(pow_done, 1)

            for i in range(NT):
                inverse_root(i, rs0)

            pool.wait_ge(ld_rows, 16)
            for i, (t, n) in enumerate(TILES):
                pool.wait_ge(h_ready, i + 1)
                pool.wait_ge(xn_done, i + 1)
                pool.tensor_tensor(h0[0:n, i, :], h0[0:n, i, :], rows[0:n, 0:DIM], ALU.add).then_inc(hb0_ready, 1)

            def step(j, par):
                if has(j, 0, PAIRS):
                    if isinstance(j, int) and j == 0:
                        pool.wait_ge(va_ready, NG)
                        pool.wait_ge(vd_ready, NG)
                    if has(j, 2, PAIRS):
                        pool.wait_ge(z_ready[1], j)
                    pool.tensor_copy(Vp[par][:, :, :], V[:, :, bass.ds(j * 128, 128)]).then_inc(vp_ready, 1)
                    for half in range(2):
                        u = slice(half * 6, half * 6 + 6)
                        pool.wait_ge(inv_ready, 2 * j + half + 1)
                        pool.wait_ge(exp_done, 12 * j + 6 * half + 6)
                        pool.tensor_tensor(P[par][:, u, :], P[par][:, u, :],
                                           rinv[:, u].unsqueeze(2).broadcast_to([GROUP, 6, UW]),
                                           ALU.mult).then_inc(p_ready, 1)

            steps(pool, step)

            for i, (t, n) in enumerate(TILES):
                inverse_root(NT + i, rs1)
            for i, (t, n) in enumerate(TILES):
                pool.wait_ge(h_ready, NT + i + 1)
                pool.wait_ge(xn_done, NT + i + 1)
                pool.tensor_tensor(h1[0:n, i, :], h1[0:n, i, :], rows[0:n, DIM:2 * DIM], ALU.add).then_inc(hb1_ready, 1)

        def transposed_hi(act, i):
            t, n = TILES[i % NT]
            act.wait_ge(xt_done, i + 1)
            bank = J_BANK[i % 2]
            act.activation(xn_hi[:, :, t:t + n], bank[:, 0:2 * 128].rearrange("p (k t) -> p k t", k=2)[:, :, 0:n],
                           ACT.Copy).then_inc(xh_done, 1)

        def relus(act, c):
            t0, t1, _, _ = FFN_CHUNKS[c]
            for f in range(FT):
                act.wait_ge(f1_done, c * FT + f + 1)
                if c * FT + f >= 2:
                    act.wait_ge(ff_ready, c * FT + f - 1)
                act.activation(hr[f % 2][:, 0:t1 - t0], B[f % 2][:, 0:t1 - t0], ACT.Relu,
                               bias=cols[:, 24 + f:25 + f]).then_inc(relu_done, 1)

        @block.scalar
        def _(act):
            act.dma_start(pos_sb[:, :], pos).then_inc(ld_small, 16)
            act.dma_start(first_sb[0:1, :], cls).then_inc(ld_small, 16)
            act.dma_start(first_sb[1:SEQ, :], tok_bias.broadcast_to([SEQ - 1, DIM])).then_inc(ld_small, 16)
            act.dma_start(cols[:, :], bias_cols).then_inc(ld_cols, 16)
            act.dma_start(rows[:, :], bias_rows.broadcast_to([128, 2 * DIM])).then_inc(ld_rows, 16)
            for i, (t, n) in enumerate(TILES):
                act.wait_ge(emb_done, i + 1)
                act.activation(h0[0:n, i, :], B[i][0:n, 0:DIM], ACT.Copy).then_inc(h_ready, 1)
                if i == 1:
                    act.wait_ge(ld_wv, 16)
                    for k in range(KD):
                        act.activation(wv_hi[:, k, :], wv_sb[:, k, :], ACT.Copy).then_inc(wvh_done, 1)
                if i >= 1:
                    transposed_hi(act, i - 1)
            transposed_hi(act, NT - 1)

            for g in range(NG):
                act.wait_ge(v_done, 2 * g + 1)
                act.activation(V[:, g, 0:512], B[(2 * g) % 4][0:GROUP, :], ACT.Copy).then_inc(va_ready, 1)
                if g < 2:
                    act.wait_ge((ld_w1, ld_w2)[g], 16)
                    if g:
                        act.wait_ge(abs_done, g)
                    else:
                        act.wait_ge(wv_ready, KD)
                    act.activation(below, (w1_sb, w2_sb)[g][:, :], ACT.Abs,
                                   accum_out=absum[:, g:g + 1]).then_inc(abs_done, 1)

            def queries(j, par):
                for c in range(2):
                    n = count(act, 4 * j + c + 1)
                    act.wait_ge(ld_cols, 16)
                    act.wait_ge(proj_done, n)
                    act.activation(QT[par][:, c * HALF:(c + 1) * HALF], J_BANK[c][:, 0:HALF], ACT.Identity,
                                   bias=cols_of(0, j)).then_inc(q_ready, 1)

            queries(0, 0)

            def step(j, par):
                for g, (t, n) in enumerate(GROUPS):
                    if has(j, 0, PAIRS):
                        for h in range(2):
                            u = 2 * g + h
                            act.wait_ge(sm_ready, 12 * j + u + 1)
                            act.activation(P[par][0:n, u, 0:n], SM[0:n, u, 0:n], ACT.Exp, bias=nmax[0:n, u:u + 1],
                                           scale=-1.0, accum_out=rsum[0:n, u:u + 1]).then_inc(exp_done, 1)
                    if has(j, 1, PAIRS + 1) and g % 2:
                        act.wait_ge(t_done, 6 * (j - 1) + g + 1)
                        act.activation(PT[1][0:n, :, 0:n],
                                       T_BANK[1][0:n, 0:2 * UW].rearrange("p (h q) -> p h q", h=2)[:, :, 0:n],
                                       ACT.Copy).then_inc(pt_ready[1], 1)
                if has(j, 0, PAIRS - 1):
                    queries(j + 1, 1 - par)

            steps(act, step)

            for i in range(NT):
                transposed_hi(act, NT + i)
                if i == NT - 2:
                    relus(act, 0)
            relus(act, 1)

        def hidden(dve, c):
            t0, t1, _, _ = FFN_CHUNKS[c]
            for f in range(FT):
                n = c * FT + f + 1
                r = hr[f % 2][:, 0:t1 - t0]
                dve.wait_ge(relu_done, n)
                dve.tensor_copy(h_hi[:, f, t0:t1], r).then_inc(hh_done, 1)
                dve.wait_ge(hh_done, n)
                dve.tensor_tensor(h_lo[:, f, t0:t1], r, h_hi[:, f, t0:t1].bitcast(F32),
                                  ALU.subtract).then_inc(ff_ready, 1)

        @block.vector
        def _(dve):
            dve.memset(ones[:, :], 1.0).then_inc(zeros_ready, 1)
            for k in range(KD):
                dve.memset(xn_hi[:, k, TOKENS:].bitcast(F32), 0.0).then_inc(zeros_ready, 1)
                dve.memset(xn_lo[:, k, TOKENS:].bitcast(F32), 0.0).then_inc(zeros_ready, 1)
            for n in range(2):
                dve.memset(P[n][:, :, :], 0.0).then_inc(zeros_ready, 1)
            dve.memset(rsum[:, :], 1.0).then_inc(zeros_ready, 1)
            for n, free in enumerate((*pt_ready, *z_ready)):
                dve.memset(rinv[:, n:n + 1], 1.0).then_inc(free, 1)
            dve.wait_ge(ld_small, 48)
            dve.tensor_tensor(first_sb[:, :], first_sb[:, :], pos_sb[:, :], ALU.add).then_inc(add_ready, 1)

            def stats(i, h):
                t = i % NT
                n = TILES[t][1]
                dve.wait_ge(h_ready, i + 1)
                dve.bn_stats(stat[0:n, t, :], h[0:n, t, :]).then_inc(stat_done, 1)
                dve.wait_ge(stat_done, i + 1)
                dve.bn_aggr(mv[0:n, t, :], stat[0:n, t, :]).then_inc(mv_done, 1)
                dve.wait_ge(mv_done, i + 1)
                dve.tensor_scalar(ve[0:n, t:t + 1], mv[0:n, t, 1:2], EPS, None, ALU.add).then_inc(ve_ready, 1)

            def normalise(i, h, rs, rt):
                t = i % NT
                n = TILES[t][1]
                r, w, v = rs[0:n, t:t + 1], rt[0:n, t:t + 1], ve[0:n, t:t + 1]
                dve.wait_ge(pow_done, i + 1)
                dve.scalar_tensor_tensor(w, r, r, v, ALU.mult, ALU.mult).then_inc(nt_a, 1)
                dve.wait_ge(nt_a, i + 1)
                dve.tensor_scalar(w, w, -0.5, 1.5, ALU.mult, ALU.add).then_inc(nt_b, 1)
                dve.wait_ge(nt_b, i + 1)
                dve.tensor_tensor(r, r, w, ALU.mult).then_inc(rstd_ready, 1)
                dve.wait_ge(rstd_ready, i + 1)
                if i >= NT:
                    dve.wait_ge(xt_done, i - NT + 1)
                dve.tensor_scalar(xn[0:n, t, :], h[0:n, t, :], mv[0:n, t, 0:1], r,
                                  ALU.subtract, ALU.mult).then_inc(xn_done, 1)

            def transposed_lo(i):
                t, n = TILES[i % NT]
                dve.wait_ge(xh_done, i + 1)
                src = J_BANK[i % 2][:, 0:2 * 128].rearrange("p (k t) -> p k t", k=2)[:, :, 0:n]
                dve.tensor_tensor(xn_lo[:, :, t:t + n], src, xn_hi[:, :, t:t + n].bitcast(F32),
                                  ALU.subtract).then_inc(xn_ready, 1)

            def split_pair(j, par):
                src = wqk_sb[:, bass.ds(j * (KD * 256), KD * 256)]
                dve.tensor_copy(wqk_hi[par][:, :], src).then_inc(wqh_done, 1)
                dve.wait_ge(wqh_done, j + 1)
                dve.tensor_tensor(wqk_lo[par][:, :], src, wqk_hi[par][:, :].bitcast(F32),
                                  ALU.subtract).then_inc(wq_ready, 1)

            for i in range(NT + 2):
                if i < NT:
                    stats(i, h0)
                if 1 <= i <= NT:
                    normalise(i - 1, h0, rs0, rt0)
                if i >= 2:
                    transposed_lo(i - 2)
                if i == 2:
                    for k in range(KD):
                        dve.wait_ge(wvh_done, k + 1)
                        dve.tensor_tensor(wv_lo[:, k, :], wv_sb[:, k, :], wv_hi[:, k, :].bitcast(F32),
                                          ALU.subtract).then_inc(wv_ready, 1)
                if i == 3:
                    dve.wait_ge(ld_wqk, 16)
                    split_pair(0, 0)

            def ternary(m):
                src, dst = ((w1_sb, w1q), (w2_sb, w2q))[m]
                if m == 0:
                    dve.wait_ge(abs_done, 2)
                else:
                    dve.wait_ge(wff_ready, 1)
                dve.tensor_scalar(below, src[:, :], gate[:, 2 + m:3 + m], None, ALU.is_lt).then_inc(below_done, 1)
                dve.wait_ge(below_done, m + 1)
                dve.scalar_tensor_tensor(dst[:, :], src[:, :], gate[:, m:m + 1], below,
                                         ALU.is_gt, ALU.subtract).then_inc(wff_ready, 1)

            for g in range(NG):
                dve.wait_ge(v_done, 2 * g + 2)
                dve.tensor_copy(V[:, g, 512:1024], B[(2 * g + 1) % 4][0:GROUP, :]).then_inc(vd_ready, 1)
                if g == 3:
                    dve.wait_ge(total_done, 1)
                    dve.tensor_scalar(gate[:, 0:2], J_BANK[0][:, 0:2], 1.0 / (DIM * FF), EPS,
                                      ALU.mult, ALU.add).then_inc(gam_done, 1)
                    dve.wait_ge(gam_done, 1)
                    dve.tensor_scalar(gate[:, 2:4], gate[:, 0:2], -0.5, None, ALU.mult).then_inc(gate_done, 1)
                    dve.wait_ge(gate_done, 1)
                    dve.tensor_scalar(gate[:, 0:2], gate[:, 0:2], 0.5, None, ALU.mult).then_inc(gate_ready, 1)
                    dve.wait_ge(gate_ready, 1)
                if g >= 4:
                    ternary(g - 4)

            def keys(j, par):
                for c in range(2):
                    dve.wait_ge(proj_done, 4 * j + c + 3)
                    if isinstance(j, int) and j == 0 and c == 0:
                        dve.wait_ge(ld_cols, 16)
                    dve.tensor_scalar(KT[par][:, c * HALF:(c + 1) * HALF], J_BANK[c][:, 0:HALF],
                                      cols_of(1, j), None, ALU.add).then_inc(k_ready, 1)

            keys(0, 0)

            def inverse_sums(j, half):
                u = slice(6 * half, 6 * half + 6)
                dve.wait_ge(exp_done, 12 * j + 6 * half + 6)
                if has(j, 1, PAIRS):
                    dve.wait_ge(p_ready, 2 * j + half - 1)
                dve.reciprocal(rinv[:, u], rsum[:, u]).then_inc(inv_ready, 1)

            def step(j, par):
                for g, (t, n) in enumerate(GROUPS):
                    if has(j, 0, PAIRS):
                        for h in range(2):
                            u = 2 * g + h
                            if has(j, 1, PAIRS):
                                dve.wait_ge(exp_done, 12 * (j - 1) + u + 1)
                            n_done = count(dve, 12 * j + u + 1)
                            dve.wait_ge(consts_ready, 3)
                            dve.wait_ge(s_done, n_done)
                            dve.tensor_tensor_reduce(
                                out=SM[0:n, u, 0:n], in0=S_BANK[h][0:n, 0:n], in1=mask[0:n, 0:n], scale=-SCALE,
                                scalar=1e38, op0=ALU.add, op1=ALU.min, accum_out=nmax[0:n, u:u + 1],
                            ).then_inc(sm_ready, 1)
                    if has(j, 1, PAIRS + 1):
                        if g % 2 == 0:
                            dve.wait_ge(t_done, 6 * (j - 1) + g + 1)
                            dve.tensor_copy(PT[0][0:n, :, 0:n],
                                            T_BANK[0][0:n, 0:2 * UW].rearrange("p (h q) -> p h q", h=2)[:, :, 0:n]
                                            ).then_inc(pt_ready[0], 1)
                        if g == 4:
                            attended(j - 1, 0)
                    if g == 2 and has(j, 0, PAIRS - 1):
                        if has(j, 1, PAIRS):
                            dve.wait_ge(proj_done, 4 * j)
                        split_pair(j + 1, 1 - par)
                    if g == 4 and has(j, 0, PAIRS):
                        inverse_sums(j, 0)
                if has(j, 0, PAIRS - 1):
                    keys(j + 1, 1 - par)
                if has(j, 1, PAIRS + 1):
                    attended(j - 1, 1)
                if has(j, 0, PAIRS):
                    inverse_sums(j, 1)

            def attended(j, half):
                a, b = ZHALF[half]
                dve.wait_ge(z_done[half], j + 1)
                dve.tensor_scalar(zT[:, bass.ds(j * TOKENS + a, b - a)], Z_BANK[half][:, 0:b - a],
                                  cols_of(2, j), None, ALU.add).then_inc(z_ready[half], 1)

            steps(dve, step)

            def residual(i):
                t, n = TILES[i]
                dve.wait_ge(o_done, i + 1)
                dve.wait_ge(hb0_ready, i + 1)
                dve.tensor_tensor(h1[0:n, i, :], B[i][0:n, 0:DIM], h0[0:n, i, :], ALU.add).then_inc(h_ready, 1)

            for i in range(NT + 2):
                if i < NT:
                    residual(i)
                    stats(NT + i, h1)
                if 1 <= i <= NT:
                    normalise(NT + i - 1, h1, rs1, rt1)
                if i >= 2:
                    transposed_lo(NT + i - 2)
                if i == NT:
                    hidden(dve, 0)
            hidden(dve, 1)
            for i, (t, n) in enumerate(TILES):
                dve.wait_ge(f2_done, i + 1)
                dve.wait_ge(hb1_ready, i + 1)
                dve.tensor_tensor(y[0:n, i, :], B[2 + i][0:n, 0:DIM], h1[0:n, i, :], ALU.add).then_inc(y_ready, 1)

        @block.tensor
        def _(pe):
            mm = nc.tensor.matmul

            def embed(i, k):
                t, n = TILES[i]
                return mm(B[i][0:n, 0:DIM], xw_sb[:, k, t:t + n], xw_sb[:, k, TOKENS:], start=(k == 0), stop=False)

            def transposes(i):
                t, n = TILES[i % NT]
                pe.wait_ge(xn_done, i + 1)
                if i % NT >= 2:
                    pe.wait_ge(xn_ready, i - 1)
                bank = J_BANK[i % 2]
                for k in range(KD):
                    last = nc.tensor.transpose(bank[:, k * 128:k * 128 + n], xn[0:n, i % NT, k * 128:k * 128 + 128],
                                               ident[0:n, 0:n])
                last.then_inc(xt_done, 1)

            def values(g):
                for half in range(2):
                    if 2 * g + half >= 4:
                        pe.wait_ge((va_ready, vd_ready)[half], g - 1)
                    c = slice(half * 512, half * 512 + 512)
                    terms = [(k, a, b) for k in range(KD) for a, b in ((xn_hi, wv_hi), (xn_hi, wv_lo), (xn_lo, wv_hi))]
                    for m, (k, a, b) in enumerate(terms):
                        last = mm(B[(2 * g + half) % 4][0:GROUP, :], a[:, k, g * GROUP:(g + 1) * GROUP], b[:, k, c],
                                  start=(m == 0), stop=(m == len(terms) - 1))
                    last.then_inc(v_done, 1)

            early = 2
            for k in range(early):
                pe.wait_ge(ld_xw[k], 16)
                for i in range(NT):
                    embed(i, k)
            for i, (t, n) in enumerate(TILES):
                for k in range(early, KP):
                    if i == 0:
                        pe.wait_ge(ld_xw[k], 16)
                    embed(i, k)
                if i == 0:
                    pe.wait_ge(add_ready, 1)
                    pe.wait_ge(consts_ready, 2)
                mm(B[i][0:n, 0:DIM], onehot[:, t:t + n], first_sb[:, :], start=False, stop=True).then_inc(emb_done, 1)
                if i >= 1:
                    transposes(i - 1)
            pe.wait_ge(zeros_ready, 8)
            pe.wait_ge(wv_ready, KD)
            pe.wait_ge(h_ready, NT)
            for g in range(NG):
                pe.wait_ge(xn_ready, min(NT, g + 1))
                if g == 1:
                    transposes(NT - 1)
                values(g)
                if g == 3:
                    pe.wait_ge(abs_done, 2)
                    pe.wait_ge(xn_ready, NT)
                    mm(J_BANK[0][:, 0:2], ones[:, :], absum[:, :], start=True, stop=True).then_inc(total_done, 1)

            def project(j, par):
                pe.wait_ge(wq_ready, j + 1)
                for c in range(4):
                    what, half = c // 2, c % 2
                    if what:
                        pe.wait_ge(q_ready, 2 * j + half + 1)
                    elif has(j, 1, PAIRS):
                        pe.wait_ge(k_ready, 2 * j + half - 1)
                    elif half == 0:
                        pe.wait_ge(gam_done, 1)
                    tok = slice(half * HALF, (half + 1) * HALF)
                    terms = [(k, a, b) for k in range(KD) for a, b in
                             ((wqk_hi[par], xn_hi), (wqk_hi[par], xn_lo), (wqk_lo[par], xn_hi))]
                    for m, (k, a, b) in enumerate(terms):
                        w = slice(k * 256 + what * 128, k * 256 + what * 128 + 128)
                        last = mm(J_BANK[half][:, 0:HALF], a[:, w], b[:, k, tok],
                                  start=(m == 0), stop=(m == len(terms) - 1))
                    last.then_inc(proj_done, 1)

            project(0, 0)

            def scores(j, par, g):
                t, n = GROUPS[g]
                if g == 0:
                    pe.wait_ge(q_ready, 2 * j + 2)
                    pe.wait_ge(k_ready, 2 * j + 2)
                for h in range(2):
                    if g >= 1 or has(j, 1, PAIRS):
                        read = count(pe, 12 * j + 2 * g + h - 1)
                        if g == NG - 1:
                            pe.wait_ge(ld_cols, 16)
                        pe.wait_ge(sm_ready, read)
                    elif h == 0:
                        pe.wait_ge(va_ready, NG)
                        pe.wait_ge(vd_ready, NG)
                    d = slice(64 * h, 64 * h + 64)
                    mm(S_BANK[h][0:n, 0:n], QT[par][d, t:t + n], KT[par][d, t:t + n],
                       start=True, stop=True).then_inc(s_done, 1)

            def probs_transposed(j, par, g):
                t, n = GROUPS[g]
                if g % 3 == 0:
                    pe.wait_ge(p_ready, 2 * j + g // 3 + 1)
                read = count(pe, 3 * j + g // 2 + 1)
                pe.wait_ge(consts_ready, 2)
                if g >= 2 or has(j, 1, PAIRS):
                    pe.wait_ge(pt_ready[g % 2], read)
                for h in range(2):
                    last = nc.tensor.transpose(T_BANK[g % 2][0:n, h * UW:h * UW + n], P[par][0:n, 2 * g + h, 0:n],
                                               ident[0:n, 0:n])
                last.then_inc(t_done, 1)

            def attend(j, par, g):
                t, n = GROUPS[g]
                half, at = g // 3, t - ZHALF[g // 3][0]
                if g == 0:
                    pe.wait_ge(vp_ready, j + 1)
                if g % 3 == 0 and has(j, 1, PAIRS):
                    pe.wait_ge(z_ready[half], j + 1)
                here = count(pe, 3 * j + g // 2 + 2)
                if g == NG - 1:
                    pe.wait_ge(ld_cols, 16)
                pe.wait_ge(pt_ready[g % 2], here)
                for h in range(2):
                    last = mm(Z_BANK[half][64 * h:64 * h + 64, at:at + n], Vp[par][0:n, g, 64 * h:64 * h + 64],
                              PT[g % 2][0:n, h, 0:n], start=True, stop=True)
                if g % 3 == 2:
                    last.then_inc(z_done[half], 1)

            def step(j, par):
                for g in range(NG + 1):
                    if g < NG:
                        if has(j, 0, PAIRS):
                            scores(j, par, g)
                        if has(j, 1, PAIRS + 1):
                            probs_transposed(j - 1, 1 - par, g)
                    if g >= 1 and has(j, 1, PAIRS + 1):
                        attend(j - 1, 1 - par, g - 1)
                if has(j, 0, PAIRS - 1):
                    project(j + 1, 1 - par)

            steps(pe, step)

            def output(i):
                t, n = TILES[i]
                for j in range(PAIRS):
                    last = mm(B[i][0:n, 0:DIM], zT[:, j * TOKENS + t:j * TOKENS + t + n], wo_sb[:, j, :],
                              start=(j == 0), stop=(j == PAIRS - 1))
                last.then_inc(o_done, 1)

            def up(c):
                t0, t1, i0, i1 = FFN_CHUNKS[c]
                pe.wait_ge(xn_ready, NT + i1)
                for f in range(FT):
                    n = c * FT + f
                    if n >= 2:
                        pe.wait_ge(relu_done, n - 1)
                    terms = [(k, b) for k in range(KD) for b in (xn_hi, xn_lo)]
                    for m, (k, b) in enumerate(terms):
                        last = mm(B[f % 2][:, 0:t1 - t0], w1q[:, k * FF + f * 128:k * FF + f * 128 + 128], b[:, k, t0:t1],
                                  start=(m == 0), stop=(m == len(terms) - 1))
                    last.then_inc(f1_done, 1)

            def down(i):
                t, n = TILES[i]
                pe.wait_ge(ff_ready, FT if i < FFN_CHUNKS[0][3] else 2 * FT)
                if i == 4:
                    pe.wait_ge(xn_ready, 2 * NT)
                for f in range(FT):
                    for m, a in enumerate((h_hi, h_lo)):
                        last = mm(B[2 + i][0:n, 0:DIM], a[:, f, t:t + n], w2q[:, f * DIM:(f + 1) * DIM],
                                  start=(f == 0 and m == 0), stop=(f == FT - 1 and m == 1))
                last.then_inc(f2_done, 1)

            pe.wait_ge(ld_wo, 16)
            pe.wait_ge(sm_ready, 12 * PAIRS)
            pe.wait_ge(z_ready[0], PAIRS + 1)
            pe.wait_ge(z_ready[1], PAIRS + 1)
            pe.wait_ge(pt_ready[0], 3 * PAIRS + 1)
            pe.wait_ge(pt_ready[1], 3 * PAIRS + 1)
            for i in range(NT):
                output(i)
                if i >= 1:
                    transposes(NT + i - 1)
            pe.wait_ge(wff_ready, 2)
            pe.wait_ge(h_ready, NT + 2)
            up(0)
            transposes(2 * NT - 1)
            up(1)
            pe.wait_ge(h_ready, 2 * NT)
            for i in range(NT):
                down(i)


def kernel(**inputs):
    import numpy as np
    import concourse.bacc as bacc
    from concourse.bass_utils import run_bass_kernel_spmd

    def two(a, width):
        return np.ascontiguousarray(a.reshape(-1, 128, width).transpose(1, 0, 2))

    g = {k: np.asarray(v) for k, v in inputs.items()}
    p = g["x"].reshape(IMAGES, 3, 6, 16, 6, 16).transpose(0, 2, 4, 1, 3, 5).reshape(IMAGES, SEQ - 1, PATCH_DIM)
    tok = np.zeros((IMAGES, SEQ, PATCH_DIM), p.dtype)
    tok[:, 1:] = p
    xt = tok.reshape(TOKENS, PATCH_DIM).T.reshape(KP, 128, TOKENS)
    wt = g["L0_tok_W"].T.reshape(KP, 128, DIM)
    wq, wk, wvt = (g[f"L0_attn_W_{n}"].reshape(HEADS * HEAD_DIM, DIM).T for n in "QKV")
    wqk = np.stack([a.reshape(KD, 128, PAIRS, 128) for a in (wq, wk)], 3)
    arrays = {
        "xw": np.ascontiguousarray(np.concatenate([xt, wt], 2)),
        "wqk": np.ascontiguousarray(wqk.transpose(1, 2, 0, 3, 4)).reshape(128, PAIRS * KD * 256),
        "wv": two(wvt, FF),
        "wo": two(g["L0_attn_W_O"].transpose(0, 2, 1).reshape(HEADS * HEAD_DIM, DIM), DIM),
        "w1": two(g["L0_ffn_W1"].T, FF).reshape(128, KD * FF),
        "w2": two(g["L0_ffn_W2"].T, DIM).reshape(128, FT * DIM),
        "bias_cols": np.ascontiguousarray(np.concatenate(
            [g[n].reshape(8, 128).T for n in ("L0_attn_b_Q", "L0_attn_b_K", "L0_attn_b_V", "L0_ffn_b1")], 1)),
        "bias_rows": np.concatenate([g["L0_attn_b_O"], g["L0_ffn_b2"]]).reshape(1, 2 * DIM),
        "tok_bias": g["L0_tok_b"].reshape(1, DIM),
        "cls": g["L0_tok_cls_token"].reshape(1, DIM),
        "pos": np.ascontiguousarray(g["L0_tok_pos_embed"].reshape(SEQ, DIM)),
    }
    nc = bacc.Bacc("TRN2", target_bir_lowering=False, num_devices=1)
    args = [nc.dram_tensor(f"in_{n}", a.shape, mybir.dt.from_np(a.dtype), kind="ExternalInput").ap()
            for n, a in arrays.items()]
    out = nc.dram_tensor("out", (TOKENS, DIM), F32, kind="ExternalOutput").ap()
    vit_block(nc, *args, out)
    r = run_bass_kernel_spmd(nc, [{f"in_{n}": a for n, a in arrays.items()}], core_ids=[0])
    return r.results[0]["out"].reshape(IMAGES, SEQ, DIM)
```

```python
import concourse.bass as bass
from concourse import mybir
from contextlib import ExitStack

F32 = mybir.dt.float32
F32R = mybir.dt.float32r
ALU = mybir.AluOpType
ACT = mybir.ActivationFunctionType
AX = mybir.AxisListType

IMAGES, SEQ, DIM = 16, 37, 256
TOKENS = IMAGES * SEQ
PATCH_DIM = 3 * 16 * 16
KP = PATCH_DIM // 128
KD = DIM // 128
HEADS, HEAD_DIM = 16, 64
PAIRS = HEADS // 2
FF = 1024
FT = FF // 128
TILES = [(t, min(128, TOKENS - t)) for t in range(0, TOKENS, 128)]
NT = len(TILES)
PER_GROUP = 128 // SEQ
GROUP = PER_GROUP * SEQ
GROUPS = [(g, min(GROUP, TOKENS - g)) for g in range(0, TOKENS, GROUP)]
NG = len(GROUPS)
UNITS = 2 * NG
UW = GROUP + 1
HALF = TOKENS // 2
ZHALF = [(0, 3 * GROUP), (3 * GROUP, TOKENS)]
FFN_CHUNKS = [(0, 256, 0, 2), (256, TOKENS, 2, NT)]
PASSES_AT = [(3, 2), (2, 2), (2, 2), (2, 2), (2, 2), (1, 2), (0, 0)]
EARLY = 4
QUERIES_AT, KEYS_AT = (1, 3), (4, 5)
EPS = 1e-5
SCALE = float(HEAD_DIM) ** -0.5
HIDDEN_KEY = -1e5 / SCALE
OTHER_IMAGE = -1e30


def vit_block(nc, xw, wqk, wv, wo, w1, w2, bias_cols, bias_rows, tok_bias, cls, pos, out):
    with ExitStack() as ctx:
        def sb(name, shape, dt=F32):
            return ctx.enter_context(nc.sbuf_tensor(name, shape, dt))

        def overlay(*specs):
            def size(spec):
                n = 1
                for d in spec[1][1:]:
                    n *= d
                return n
            held = max(range(len(specs)), key=lambda i: size(specs[i]))
            tensors = {}
            for i, spec in enumerate(specs):
                if i != held:
                    with nc.sbuf_tensor(*spec) as tensors[i]:
                        pass
            tensors[held] = sb(*specs[held])
            return [tensors[i] for i in range(len(specs))]

        def sem(name):
            return ctx.enter_context(nc.semaphore(name))

        XW = [128, KP, TOKENS + DIM]
        xw_sb, attn = overlay(("xw_sb", XW, F32), ("attn", [128, 3 * UNITS * UW], F32))
        xw_hi, z_hi = overlay(("xw_hi", XW, F32R), ("z_hi", [128, PAIRS * TOKENS], F32R))
        xw_lo, V, h_lo = overlay(("xw_lo", XW, F32R), ("V", [128, NG, FF], F32), ("h_lo", [128, FT, TOKENS], F32R))
        wqk_sb, h_hi = overlay(("wqk_sb", [128, (PAIRS + 1) * KD * 256], F32), ("h_hi", [128, FT, TOKENS], F32R))
        wv_sb = sb("wv_sb", [128, KD, FF])
        wv_split, z_lo = overlay(("wv_split", [128, 2 * KD, FF], F32R), ("z_lo", [128, PAIRS * TOKENS], F32R))
        wv_hi, wv_lo = wv_split[:, 0:KD, :], wv_split[:, KD:2 * KD, :]
        wo_sb = sb("wo_sb", [128, PAIRS * DIM])
        w1_sb, wo_hi = overlay(("w1_sb", [128, KD * FF], F32), ("wo_hi", [128, PAIRS * DIM], F32R))
        w2_sb, wo_lo = overlay(("w2_sb", [128, FT * DIM], F32), ("wo_lo", [128, PAIRS * DIM], F32R))
        cols = sb("cols", [128, 4 * 8])
        rows = sb("rows", [128, 2 * DIM])
        pos_sb, xn = overlay(("pos_sb", [SEQ, DIM], F32), ("xn", [128, NT, DIM], F32))
        first_sb = sb("first_sb", [SEQ, DIM])
        ident = sb("ident", [128, 128])
        first_hi, first_lo = sb("first_hi", [SEQ, DIM], F32R), sb("first_lo", [SEQ, DIM], F32R)
        onehot, pt = overlay(("onehot", [SEQ, TOKENS], F32R), ("pt", [GROUP, 4 * UW], F32))
        mask = sb("mask", [GROUP, UW])
        ones = sb("ones", [128, 128])
        power = sb("power", [128, 1])
        wqk_hi = [sb(f"wqk_hi{n}", [128, KD * 256], F32R) for n in range(2)]
        wqk_lo = [sb(f"wqk_lo{n}", [128, KD * 256], F32R) for n in range(2)]
        w1q, w2q = sb("w1q", [128, KD * FF], F32R), sb("w2q", [128, FT * DIM], F32R)
        below = wv_sb[:, :, :].rearrange("p k n -> p (k n)")
        absum = sb("absum", [128, 2])
        gate = sb("gate", [128, 4])
        h0 = sb("h0", [128, NT, DIM])
        h1 = sb("h1", [128, NT, DIM])
        stat = sb("stat", [128, NT, 6])
        mv = sb("mv", [128, NT, 2])
        ve = sb("ve", [128, NT])
        rs0, rs1 = sb("rs0", [128, NT]), sb("rs1", [128, NT])
        rt0, rt1 = sb("rt0", [128, NT]), sb("rt1", [128, NT])
        XC = GROUP * NG
        xn_hi, xn_lo = sb("xn_hi", [128, KD, XC], F32R), sb("xn_lo", [128, KD, XC], F32R)
        V = V[0:GROUP, :, :]
        Vp = [sb(f"Vp{n}", [GROUP, NG, 128]) for n in range(2)]
        HR = max(b - a for a, b, _, _ in FFN_CHUNKS)
        qk, late = overlay(("qk", [128, 4 * TOKENS], F32), ("late", [128, 2 * HR + NT * DIM], F32))
        QT = [qk[:, n * TOKENS:(n + 1) * TOKENS] for n in (0, 1)]
        KT = [qk[:, n * TOKENS:(n + 1) * TOKENS] for n in (2, 3)]
        hr = [late[:, n * HR:(n + 1) * HR] for n in range(2)]
        y = late[:, 2 * HR:].rearrange("p (i n) -> p i n", n=DIM)
        by_unit = attn[0:GROUP, :].rearrange("p (a u c) -> p a u c", a=3, c=UW)
        P = [by_unit[:, 0], by_unit[:, 1]]
        SM = by_unit[:, 2]
        nmax = sb("nmax", [GROUP, UNITS])
        rsum = sb("rsum", [GROUP, UNITS])
        rinv = sb("rinv", [GROUP, UNITS])
        PT = [pt[:, n * 2 * UW:(n + 1) * 2 * UW].rearrange("p (h q) -> p h q", h=2) for n in range(2)]

        B = [ctx.enter_context(nc.psum_tensor(f"bank{n}", [128, 512], F32)) for n in range(8)]
        S_BANK, T_BANK, Z_BANK, J_BANK = B[0:2], B[2:4], B[4:6], B[6:8]
        XT_BANK = [B[6:8], [B[3], B[5]]]
        O_BANK = [B[6], B[7], B[0], B[1], B[2]]
        U_BANK = [B[4], B[6], B[7]]
        D_BANK = [B[0], B[1], B[2], B[3], B[5]]

        ld_xw = [sem(f"ld_xw{k}") for k in range(KP)]
        ld_small, ld_cols, ld_rows = sem("ld_small"), sem("ld_cols"), sem("ld_rows")
        ld_wqk, ld_wv, ld_wo, ld_w1, ld_w2 = (sem(f"ld_{n}") for n in ("wqk", "wv", "wo", "w1", "w2"))
        filled = sem("filled")
        consts_ready = sem("consts_ready")
        zeros_ready = sem("zeros_ready")
        add_ready = sem("add_ready")
        xwh_done, xw_ready = sem("xwh_done"), sem("xw_ready")
        fh_done, first_ready = sem("fh_done"), sem("first_ready")
        woh_done, wo_ready = sem("woh_done"), sem("wo_ready")
        emb_done = sem("emb_done")
        h_ready = sem("h_ready")
        stat_done, mv_done, ve_ready = sem("stat_done"), sem("mv_done"), sem("ve_ready")
        pow_done, nt_a, nt_b, rstd_ready = sem("pow_done"), sem("nt_a"), sem("nt_b"), sem("rstd_ready")
        xn_done = sem("xn_done")
        xt_done = sem("xt_done")
        xh_done, xn_ready = sem("xh_done"), sem("xn_ready")
        wvh_done, wv_ready = sem("wvh_done"), sem("wv_ready")
        wqh_done, wq_ready = sem("wqh_done"), sem("wq_ready")
        abs_done, total_done, gam_done, gate_done, gate_ready = (
            sem(n) for n in ("abs_done", "total_done", "gam_done", "gate_done", "gate_ready"))
        below_done, wff_ready = sem("below_done"), sem("wff_ready")
        v_done = sem("v_done")
        va_ready, vd_ready = sem("va_ready"), sem("vd_ready")
        vp_ready = sem("vp_ready")
        proj_done = sem("proj_done")
        q_ready, k_ready = sem("q_ready"), sem("k_ready")
        s_done, sm_ready, exp_done = sem("s_done"), sem("sm_ready"), sem("exp_done")
        inv_ready, p_ready = sem("inv_ready"), sem("p_ready")
        t_done = sem("t_done")
        pt_ready = [sem("pt_even_ready"), sem("pt_odd_ready")]
        z_done, z_ready = [sem("z0_done"), sem("z1_done")], [sem("z0_ready"), sem("z1_ready")]
        zh_done = [sem("zh0_done"), sem("zh1_done")]
        hb0_ready, hb1_ready = sem("hb0_ready"), sem("hb1_ready")
        o_done = sem("o_done")
        f1_done, relu_done, hh_done, ff_ready = sem("f1_done"), sem("relu_done"), sem("hh_done"), sem("ff_ready")
        f2_done, y_ready, stored = sem("f2_done"), sem("y_ready"), sem("stored")

        block = ctx.enter_context(nc.Block())

        def cols_of(group_units, j):
            return cols[:, bass.ds(group_units * 8 + j, 1)]

        def steps(eng, step):
            step(0, 0)
            with eng.Fori(0, PAIRS // 2 - 1) as twice:
                step(twice * 2 + 1, 1)
                step(twice * 2 + 2, 0)
            step(PAIRS - 1, 1)
            step(PAIRS, 0)

        def count(eng, value):
            if not isinstance(value, int):
                eng.lower_val(value)
            return value

        def has(j, lo, hi):
            return lo <= j < hi if isinstance(j, int) else True

        @block.sync
        def _(sp):
            for k in range(KP):
                sp.dma_start(xw_sb[:, k, :], xw[k]).then_inc(ld_xw[k], 16)
            sp.dma_start(wv_sb[:, :, :], wv).then_inc(ld_wv, 16)
            sp.dma_start(w1_sb[:, :], w1).then_inc(ld_w1, 16)
            sp.dma_start(w2_sb[:, :], w2).then_inc(ld_w2, 16)
            sp.dma_start(wqk_sb[:, 0:PAIRS * KD * 256], wqk).then_inc(ld_wqk, 16)
            sp.dma_start(wo_sb[:, :], wo).then_inc(ld_wo, 16)
            for i, (t, n) in enumerate(TILES):
                sp.wait_ge(y_ready, i + 1)
                sp.dma_start(out[t:t + n, :], y[0:n, i, :]).then_inc(stored, 16)
            sp.wait_ge(stored, 16 * NT)

        @block.gpsimd
        def _(pool):
            pool.memset(onehot[:, :].bitcast(F32), 0.0).then_inc(filled, 1)
            pool.memset(ident[:, :], 0.0).then_inc(filled, 1)
            pool.memset(mask[:, :], 0.0).then_inc(filled, 1)
            pool.memset(power[:, :], -0.5).then_inc(filled, 1)
            pool.wait_ge(filled, 4)
            pool.affine_select(out=onehot[:, :], in_=onehot[:, :].bitcast(F32), compare_op=ALU.not_equal, fill=1.0, base=0,
                               pattern=[[0, IMAGES], [-1, SEQ]], channel_multiplier=1).then_inc(consts_ready, 1)
            pool.affine_select(out=ident[:, :], in_=ident[:, :], compare_op=ALU.not_equal, fill=1.0, base=0,
                               pattern=[[-1, 128]], channel_multiplier=1).then_inc(consts_ready, 1)
            mk = mask[:, 0:GROUP]
            pool.affine_select(out=mk, in_=mk, compare_op=ALU.is_ge, fill=HIDDEN_KEY, base=0,
                               pattern=[[-1, GROUP]], channel_multiplier=1).then_inc(filled, 1)
            pool.wait_ge(filled, 5)
            pool.affine_select(out=mk, in_=mk, compare_op=ALU.is_ge, fill=OTHER_IMAGE, base=0,
                               pattern=[[-SEQ, PER_GROUP], [0, SEQ]], channel_multiplier=1).then_inc(filled, 1)
            pool.wait_ge(filled, 6)
            pool.affine_select(out=mk, in_=mk, compare_op=ALU.is_ge, fill=OTHER_IMAGE, base=SEQ - 1,
                               pattern=[[SEQ, PER_GROUP], [0, SEQ]], channel_multiplier=-1).then_inc(consts_ready, 1)

            def inverse_root(i, rs):
                pool.wait_ge(ve_ready, i + 1)
                t = i % NT
                n = TILES[t][1]
                pool.tensor_tensor(rs[0:n, t:t + 1], ve[0:n, t:t + 1], power[0:n, :], ALU.pow).then_inc(pow_done, 1)

            for i in range(NT):
                inverse_root(i, rs0)

            pool.wait_ge(ld_rows, 16)
            for i, (t, n) in enumerate(TILES):
                pool.wait_ge(h_ready, i + 1)
                pool.wait_ge(xn_done, i + 1)
                pool.tensor_tensor(h0[0:n, i, :], h0[0:n, i, :], rows[0:n, 0:DIM], ALU.add).then_inc(hb0_ready, 1)

            def step(j, par):
                if has(j, 0, PAIRS):
                    if isinstance(j, int) and j == 0:
                        pool.wait_ge(va_ready, NG)
                        pool.wait_ge(vd_ready, NG)
                    if has(j, 2, PAIRS):
                        pool.wait_ge(z_ready[1], j)
                    pool.tensor_copy(Vp[par][:, :, :], V[:, :, bass.ds(j * 128, 128)]).then_inc(vp_ready, 1)
                    for half, units, n in ((0, slice(0, 6), GROUP), (1, slice(6, 10), GROUP), (1, slice(10, 12), SEQ)):
                        pool.wait_ge(inv_ready, 2 * j + half + 1)
                        pool.wait_ge(exp_done, 12 * j + units.stop)
                        p = P[par][0:n, units, 0:n]
                        pool.tensor_tensor(p, p, rinv[0:n, units].unsqueeze(2).broadcast_to(list(p.shape)),
                                           ALU.mult).then_inc(p_ready, 1)

            steps(pool, step)

            for i, (t, n) in enumerate(TILES):
                inverse_root(NT + i, rs1)
            for i, (t, n) in enumerate(TILES):
                pool.wait_ge(h_ready, NT + i + 1)
                pool.wait_ge(xn_done, NT + i + 1)
                pool.tensor_tensor(h1[0:n, i, :], h1[0:n, i, :], rows[0:n, DIM:2 * DIM], ALU.add).then_inc(hb1_ready, 1)

        def transposed_hi(act, i):
            t, n = TILES[i % NT]
            act.wait_ge(xt_done, i + 1)
            bank = XT_BANK[i // NT][i % 2]
            act.activation(xn_hi[:, :, t:t + n], bank[:, 0:2 * 128].rearrange("p (k t) -> p k t", k=2)[:, :, 0:n],
                           ACT.Copy).then_inc(xh_done, 1)

        def relus(act, c, f0, f1):
            t0, t1, _, _ = FFN_CHUNKS[c]
            for f in range(f0, f1):
                act.wait_ge(f1_done, c * FT + f + 1)
                if c * FT + f >= 2:
                    act.wait_ge(ff_ready, c * FT + f - 1)
                act.activation(hr[f % 2][:, 0:t1 - t0], U_BANK[(c * FT + f) % 3][:, 0:t1 - t0], ACT.Relu,
                               bias=cols[:, 24 + f:25 + f]).then_inc(relu_done, 1)

        @block.scalar
        def _(act):
            act.dma_start(pos_sb[:, :], pos).then_inc(ld_small, 16)
            act.dma_start(first_sb[0:1, :], cls).then_inc(ld_small, 16)
            act.dma_start(first_sb[1:SEQ, :], tok_bias.broadcast_to([SEQ - 1, DIM])).then_inc(ld_small, 16)
            act.dma_start(cols[:, :], bias_cols).then_inc(ld_cols, 16)
            act.dma_start(rows[:, :], bias_rows.broadcast_to([128, 2 * DIM])).then_inc(ld_rows, 16)
            for k in range(KP):
                act.wait_ge(ld_xw[k], 16)
                act.activation(xw_hi[:, k, :], xw_sb[:, k, :], ACT.Copy).then_inc(xwh_done, 1)
            for i, (t, n) in enumerate(TILES):
                act.wait_ge(emb_done, i + 1)
                act.activation(h0[0:n, i, :], B[i][0:n, 0:DIM], ACT.Copy).then_inc(h_ready, 1)
                if i < KD:
                    act.wait_ge(ld_wv, 16)
                    act.activation(wv_hi[:, i, :], wv_sb[:, i, :], ACT.Copy).then_inc(wvh_done, 1)
                if i >= 2:
                    transposed_hi(act, i - 2)

            for g in range(NG):
                if g < 2:
                    transposed_hi(act, NT - 2 + g)
                act.wait_ge(v_done, 2 * g + 1)
                act.activation(V[:, g, 0:512], B[(2 * g) % 4][0:GROUP, :], ACT.Copy).then_inc(va_ready, 1)
                if g == 5:
                    act.wait_ge(wff_ready, 1)
                    act.wait_ge(ld_wo, 16)
                    act.activation(wo_hi[:, :], wo_sb[:, :], ACT.Copy).then_inc(woh_done, 1)
                if g < 2:
                    act.wait_ge((ld_w1, ld_w2)[g], 16)
                    if g:
                        act.wait_ge(abs_done, g)
                    else:
                        act.wait_ge(wv_ready, KD)
                    act.activation(below, (w1_sb, w2_sb)[g][:, :], ACT.Abs,
                                   accum_out=absum[:, g:g + 1]).then_inc(abs_done, 1)

            def queries(j, par, c):
                n = count(act, 4 * j + c + 1)
                act.wait_ge(ld_cols, 16)
                act.wait_ge(proj_done, n)
                act.activation(QT[par][:, c * HALF:(c + 1) * HALF], J_BANK[c][:, 0:HALF], ACT.Identity,
                               bias=cols_of(0, j)).then_inc(q_ready, 1)

            queries(0, 0, 0)
            queries(0, 0, 1)

            def attended_hi(j, half):
                a, b = ZHALF[half]
                n = count(act, j + 1)
                act.wait_ge(ld_cols, 16)
                act.wait_ge(z_done[half], n)
                act.activation(z_hi[:, bass.ds(j * TOKENS + a, b - a)], Z_BANK[half][:, 0:b - a], ACT.Identity,
                               bias=cols_of(2, j)).then_inc(zh_done[half], 1)

            def step(j, par):
                for g, (t, n) in enumerate(GROUPS):
                    if g == 4 and has(j, 1, PAIRS + 1):
                        attended_hi(j - 1, 0)
                    if has(j, 1, PAIRS + 1) and g % 2:
                        act.wait_ge(t_done, 6 * (j - 1) + g + 1)
                        act.activation(PT[1][0:n, :, 0:n],
                                       T_BANK[1][0:n, 0:2 * UW].rearrange("p (h q) -> p h q", h=2)[:, :, 0:n],
                                       ACT.Copy).then_inc(pt_ready[1], 1)
                    if g in QUERIES_AT and has(j, 0, PAIRS - 1):
                        queries(j + 1, 1 - par, QUERIES_AT.index(g))
                    if has(j, 0, PAIRS):
                        for h in range(2):
                            u = 2 * g + h
                            act.wait_ge(sm_ready, 12 * j + u + 1)
                            act.activation(P[par][0:n, u, 0:n], SM[0:n, u, 0:n], ACT.Exp, bias=nmax[0:n, u:u + 1],
                                           scale=-1.0, accum_out=rsum[0:n, u:u + 1]).then_inc(exp_done, 1)

                if has(j, 1, PAIRS + 1):
                    attended_hi(j - 1, 1)

            steps(act, step)

            for i in range(NT - 2):
                transposed_hi(act, NT + i)
            relus(act, 0, 0, FT // 2)
            transposed_hi(act, 2 * NT - 2)
            relus(act, 0, FT // 2, FT)
            transposed_hi(act, 2 * NT - 1)
            relus(act, 1, 0, FT)

        def hidden(dve, c, f0, f1):
            t0, t1, _, _ = FFN_CHUNKS[c]
            for f in range(f0, f1):
                n = c * FT + f + 1
                r = hr[f % 2][:, 0:t1 - t0]
                dve.wait_ge(relu_done, n)
                dve.tensor_copy(h_hi[:, f, t0:t1], r).then_inc(hh_done, 1)
                dve.wait_ge(hh_done, n)
                dve.tensor_tensor(h_lo[:, f, t0:t1], r, h_hi[:, f, t0:t1].bitcast(F32),
                                  ALU.subtract).then_inc(ff_ready, 1)

        @block.vector
        def _(dve):
            dve.memset(ones[:, :], 1.0).then_inc(zeros_ready, 1)
            dve.memset(wqk_sb[:, PAIRS * KD * 256:], 0.0).then_inc(zeros_ready, 1)
            for k in range(KD):
                dve.memset(xn_hi[:, k, TOKENS:].bitcast(F32), 0.0).then_inc(zeros_ready, 1)
                dve.memset(xn_lo[:, k, TOKENS:].bitcast(F32), 0.0).then_inc(zeros_ready, 1)
            dve.memset(rsum[:, :], 1.0).then_inc(zeros_ready, 1)
            for n, free in enumerate((*pt_ready, *z_ready)):
                dve.memset(rinv[:, n:n + 1], 1.0).then_inc(free, 1)
            for k in range(KP):
                dve.wait_ge(xwh_done, k + 1)
                dve.tensor_tensor(xw_lo[:, k, :], xw_sb[:, k, :], xw_hi[:, k, :].bitcast(F32),
                                  ALU.subtract).then_inc(xw_ready, 1)
                if k == 1:
                    dve.wait_ge(ld_small, 48)
                    dve.tensor_tensor(first_sb[:, :], first_sb[:, :], pos_sb[:, :], ALU.add).then_inc(add_ready, 1)
                    dve.wait_ge(add_ready, 1)
                    dve.tensor_copy(first_hi[:, :], first_sb[:, :]).then_inc(fh_done, 1)
                    dve.wait_ge(fh_done, 1)
                    dve.tensor_tensor(first_lo[:, :], first_sb[:, :], first_hi[:, :].bitcast(F32),
                                      ALU.subtract).then_inc(first_ready, 1)

            def stats(i, h):
                t = i % NT
                n = TILES[t][1]
                dve.wait_ge(h_ready, i + 1)
                dve.bn_stats(stat[0:n, t, :], h[0:n, t, :]).then_inc(stat_done, 1)
                dve.wait_ge(stat_done, i + 1)
                dve.bn_aggr(mv[0:n, t, :], stat[0:n, t, :]).then_inc(mv_done, 1)
                dve.wait_ge(mv_done, i + 1)
                dve.tensor_scalar(ve[0:n, t:t + 1], mv[0:n, t, 1:2], EPS, None, ALU.add).then_inc(ve_ready, 1)

            def normalise(i, h, rs, rt):
                t = i % NT
                n = TILES[t][1]
                r, w, v = rs[0:n, t:t + 1], rt[0:n, t:t + 1], ve[0:n, t:t + 1]
                dve.wait_ge(pow_done, i + 1)
                dve.scalar_tensor_tensor(w, r, r, v, ALU.mult, ALU.mult).then_inc(nt_a, 1)
                dve.wait_ge(nt_a, i + 1)
                dve.tensor_scalar(w, w, -0.5, 1.5, ALU.mult, ALU.add).then_inc(nt_b, 1)
                dve.wait_ge(nt_b, i + 1)
                dve.tensor_tensor(r, r, w, ALU.mult).then_inc(rstd_ready, 1)
                dve.wait_ge(rstd_ready, i + 1)
                if i >= NT:
                    dve.wait_ge(xt_done, i - NT + 1)
                dve.tensor_scalar(xn[0:n, t, :], h[0:n, t, :], mv[0:n, t, 0:1], r,
                                  ALU.subtract, ALU.mult).then_inc(xn_done, 1)

            def transposed_lo(i):
                t, n = TILES[i % NT]
                dve.wait_ge(xh_done, i + 1)
                src = XT_BANK[i // NT][i % 2][:, 0:2 * 128].rearrange("p (k t) -> p k t", k=2)[:, :, 0:n]
                dve.tensor_tensor(xn_lo[:, :, t:t + n], src, xn_hi[:, :, t:t + n].bitcast(F32),
                                  ALU.subtract).then_inc(xn_ready, 1)

            def split_pair(j, par):
                src = wqk_sb[:, bass.ds(j * (KD * 256), KD * 256)]
                dve.tensor_copy(wqk_hi[par][:, :], src).then_inc(wqh_done, 1)
                dve.wait_ge(wqh_done, j + 1)
                dve.tensor_tensor(wqk_lo[par][:, :], src, wqk_hi[par][:, :].bitcast(F32),
                                  ALU.subtract).then_inc(wq_ready, 1)

            for i in range(NT + 1):
                if i < NT:
                    stats(i, h0)
                if i >= 1:
                    normalise(i - 1, h0, rs0, rt0)
                if 2 <= i < NT:
                    transposed_lo(i - 2)
                if i in (2, 3):
                    k = i - 2
                    dve.wait_ge(wvh_done, k + 1)
                    dve.tensor_tensor(wv_lo[:, k, :], wv_sb[:, k, :], wv_hi[:, k, :].bitcast(F32),
                                      ALU.subtract).then_inc(wv_ready, 1)

            def ternary(m):
                src, dst = ((w1_sb, w1q), (w2_sb, w2q))[m]
                if m == 0:
                    dve.wait_ge(abs_done, 2)
                else:
                    dve.wait_ge(wff_ready, 1)
                dve.tensor_scalar(below, src[:, :], gate[:, 2 + m:3 + m], None, ALU.is_lt).then_inc(below_done, 1)
                dve.wait_ge(below_done, m + 1)
                dve.scalar_tensor_tensor(dst[:, :], src[:, :], gate[:, m:m + 1], below,
                                         ALU.is_gt, ALU.subtract).then_inc(wff_ready, 1)

            for g in range(NG):
                if g < 2:
                    transposed_lo(NT - 2 + g)
                dve.wait_ge(v_done, 2 * g + 2)
                dve.tensor_copy(V[:, g, 512:1024], B[(2 * g + 1) % 4][0:GROUP, :]).then_inc(vd_ready, 1)
                if g == 1:
                    dve.wait_ge(ld_wqk, 16)
                    split_pair(0, 0)
                    split_pair(1, 1)
                if g == 2:
                    dve.wait_ge(total_done, 1)
                    dve.tensor_scalar(gate[:, 0:2], J_BANK[0][:, 0:2], 1.0 / (DIM * FF), EPS,
                                      ALU.mult, ALU.add).then_inc(gam_done, 1)
                    dve.wait_ge(gam_done, 1)
                    dve.tensor_scalar(gate[:, 2:4], gate[:, 0:2], -0.5, None, ALU.mult).then_inc(gate_done, 1)
                    dve.wait_ge(gate_done, 1)
                    dve.tensor_scalar(gate[:, 0:2], gate[:, 0:2], 0.5, None, ALU.mult).then_inc(gate_ready, 1)
                    dve.wait_ge(gate_ready, 1)
                if g in (2, 3):
                    ternary(g - 2)

            def keys(j, par, c):
                dve.wait_ge(proj_done, 4 * j + c + 3)
                if isinstance(j, int) and j == 0 and c == 0:
                    dve.wait_ge(ld_cols, 16)
                dve.tensor_scalar(KT[par][:, c * HALF:(c + 1) * HALF], J_BANK[c][:, 0:HALF],
                                  cols_of(1, j), None, ALU.add).then_inc(k_ready, 1)

            keys(0, 0, 0)
            keys(0, 0, 1)

            def inverse_sums(j, half):
                u = slice(6 * half, 6 * half + 6)
                dve.wait_ge(exp_done, 12 * j + 6 * half + 6)
                if has(j, 1, PAIRS):
                    dve.wait_ge(p_ready, 3 * j - 2 + 2 * half)
                dve.reciprocal(rinv[:, u], rsum[:, u]).then_inc(inv_ready, 1)

            def masked_scores(j, g):
                t, n = GROUPS[g]
                for h in range(2):
                    u = 2 * g + h
                    if has(j, 1, PAIRS):
                        dve.wait_ge(exp_done, 12 * (j - 1) + u + 1)
                    n_done = count(dve, 12 * j + u + 1)
                    dve.wait_ge(consts_ready, 3)
                    dve.wait_ge(s_done, n_done)
                    dve.tensor_tensor_reduce(
                        out=SM[0:n, u, 0:n], in0=S_BANK[h][0:n, 0:n], in1=mask[0:n, 0:n], scale=-SCALE,
                        scalar=1e38, op0=ALU.add, op1=ALU.min, accum_out=nmax[0:n, u:u + 1],
                    ).then_inc(sm_ready, 1)

            def step(j, par):
                for g, (t, n) in enumerate(GROUPS):
                    if has(j, 1, PAIRS + 1) and g % 2 == 0:
                        dve.wait_ge(t_done, 6 * (j - 1) + g + 1)
                        dve.tensor_copy(PT[0][0:n, :, 0:n],
                                        T_BANK[0][0:n, 0:2 * UW].rearrange("p (h q) -> p h q", h=2)[:, :, 0:n]
                                        ).then_inc(pt_ready[0], 1)
                    if has(j, 0, PAIRS):
                        masked_scores(j, g)
                    if g == 0 and has(j, 0, PAIRS - 1):
                        dve.wait_ge(proj_done, 4 * (j + 1))
                        if has(j, 0, PAIRS - 2):
                            split_pair(j + 2, par)
                    if g == 4 and has(j, 1, PAIRS + 1):
                        attended_lo(j - 1, 0)
                    if g == 4 and isinstance(j, int) and j == 0:
                        dve.wait_ge(wff_ready, 2)
                        dve.wait_ge(woh_done, 1)
                        dve.tensor_tensor(wo_lo[:, :], wo_sb[:, :], wo_hi[:, :].bitcast(F32),
                                          ALU.subtract).then_inc(wo_ready, 1)
                    if g in KEYS_AT and has(j, 0, PAIRS - 1):
                        keys(j + 1, 1 - par, KEYS_AT.index(g))
                    if g == 3 and has(j, 0, PAIRS):
                        inverse_sums(j, 0)
                if has(j, 1, PAIRS + 1):
                    attended_lo(j - 1, 1)
                if has(j, 0, PAIRS):
                    inverse_sums(j, 1)

            def attended_lo(j, half):
                a, b = ZHALF[half]
                at = bass.ds(j * TOKENS + a, b - a)
                n = count(dve, j + 1)
                dve.wait_ge(ld_cols, 16)
                dve.wait_ge(zh_done[half], n)
                dve.scalar_tensor_tensor(z_lo[:, at], Z_BANK[half][:, 0:b - a], cols_of(2, j), z_hi[:, at].bitcast(F32),
                                         ALU.add, ALU.subtract).then_inc(z_ready[half], 1)

            steps(dve, step)

            def residual(i):
                t, n = TILES[i]
                dve.wait_ge(o_done, i + 1)
                dve.wait_ge(hb0_ready, i + 1)
                dve.tensor_tensor(h1[0:n, i, :], O_BANK[i][0:n, 0:DIM], h0[0:n, i, :], ALU.add).then_inc(h_ready, 1)

            for i in range(NT):
                residual(i)
                stats(NT + i, h1)
                if i >= 2:
                    transposed_lo(NT + i - 2)
                normalise(NT + i, h1, rs1, rt1)
            hidden(dve, 0, 0, FT // 2)
            transposed_lo(2 * NT - 2)
            hidden(dve, 0, FT // 2, FT)
            transposed_lo(2 * NT - 1)
            hidden(dve, 1, 0, FT)
            for i, (t, n) in enumerate(TILES):
                dve.wait_ge(f2_done, i + 1)
                dve.wait_ge(hb1_ready, i + 1)
                dve.tensor_tensor(y[0:n, i, :], D_BANK[i][0:n, 0:DIM], h1[0:n, i, :], ALU.add).then_inc(y_ready, 1)

        @block.tensor
        def _(pe):
            mm = nc.tensor.matmul

            def embed(i, k):
                t, n = TILES[i]
                for m, (a, b) in enumerate(((xw_hi, xw_hi), (xw_hi, xw_lo), (xw_lo, xw_hi))):
                    mm(B[i][0:n, 0:DIM], a[:, k, t:t + n], b[:, k, TOKENS:], start=(k == 0 and m == 0), stop=False)

            def transposes(i):
                t, n = TILES[i % NT]
                pe.wait_ge(xn_done, i + 1)
                if i % NT >= 2:
                    pe.wait_ge(xn_ready, i - 1)
                bank = XT_BANK[i // NT][i % 2]
                for k in range(KD):
                    last = nc.tensor.transpose(bank[:, k * 128:k * 128 + n], xn[0:n, i % NT, k * 128:k * 128 + 128],
                                               ident[0:n, 0:n])
                last.then_inc(xt_done, 1)

            def values(g):
                for half in range(2):
                    if 2 * g + half >= 4:
                        pe.wait_ge((va_ready, vd_ready)[half], g - 1)
                    c = slice(half * 512, half * 512 + 512)
                    terms = [(k, a, b) for k in range(KD) for a, b in ((xn_hi, wv_hi), (xn_hi, wv_lo), (xn_lo, wv_hi))]
                    for m, (k, a, b) in enumerate(terms):
                        last = mm(B[(2 * g + half) % 4][0:GROUP, :], a[:, k, g * GROUP:(g + 1) * GROUP], b[:, k, c],
                                  start=(m == 0), stop=(m == len(terms) - 1))
                    last.then_inc(v_done, 1)

            for k in range(EARLY):
                pe.wait_ge(xw_ready, k + 1)
                for i in range(NT):
                    embed(i, k)
            for i, (t, n) in enumerate(TILES):
                for k in range(EARLY, KP):
                    if i == 0:
                        pe.wait_ge(xw_ready, k + 1)
                    embed(i, k)
                if i == 0:
                    pe.wait_ge(first_ready, 1)
                    pe.wait_ge(consts_ready, 2)
                mm(B[i][0:n, 0:DIM], onehot[:, t:t + n], first_hi[:, :], start=False, stop=False)
                mm(B[i][0:n, 0:DIM], onehot[:, t:t + n], first_lo[:, :], start=False, stop=True).then_inc(emb_done, 1)
                if i >= 2:
                    transposes(i - 2)
            pe.wait_ge(zeros_ready, 7)
            pe.wait_ge(wv_ready, KD)
            pe.wait_ge(h_ready, NT)
            for g in range(NG):
                pe.wait_ge(xn_ready, min(NT, g + 1))
                values(g)
                if g < 2:
                    transposes(NT - 2 + g)
                if g == 2:
                    pe.wait_ge(abs_done, 2)
                    pe.wait_ge(xn_ready, NT)
                    mm(J_BANK[0][:, 0:2], ones[:, :], absum[:, :], start=True, stop=True).then_inc(total_done, 1)

            def projection(j, par):
                for c in range(4):
                    what, half = c // 2, c % 2
                    if c == 0:
                        pe.wait_ge(wq_ready, j + 1)
                    if what:
                        pe.wait_ge(q_ready, 2 * j + half + 1)
                    elif has(j, 1, PAIRS):
                        pe.wait_ge(k_ready, 2 * j + half - 1)
                    elif half == 0:
                        pe.wait_ge(gam_done, 1)
                    tok = slice(half * HALF, (half + 1) * HALF)
                    terms = [(k, a, b) for k in range(KD) for a, b in
                             ((wqk_hi[par], xn_hi), (wqk_hi[par], xn_lo), (wqk_lo[par], xn_hi))]
                    for m, (k, a, b) in enumerate(terms):
                        w = slice(k * 256 + what * 128, k * 256 + what * 128 + 128)
                        last = mm(J_BANK[half][:, 0:HALF], a[:, w], b[:, k, tok],
                                  start=(m == 0), stop=(m == len(terms) - 1))
                        if m == len(terms) - 1:
                            last.then_inc(proj_done, 1)
                        yield

            for _ in projection(0, 0):
                pass

            def scores(j, par, g):
                t, n = GROUPS[g]
                if g == 0:
                    pe.wait_ge(q_ready, 2 * j + 2)
                    pe.wait_ge(k_ready, 2 * j + 2)
                for h in range(2):
                    if g >= 1 or has(j, 1, PAIRS):
                        read = count(pe, 12 * j + 2 * g + h - 1)
                        if g == NG - 1:
                            pe.wait_ge(ld_cols, 16)
                        pe.wait_ge(sm_ready, read)
                    elif h == 0:
                        pe.wait_ge(va_ready, NG)
                        pe.wait_ge(vd_ready, NG)
                    d = slice(64 * h, 64 * h + 64)
                    mm(S_BANK[h][0:n, 0:n], QT[par][d, t:t + n], KT[par][d, t:t + n],
                       start=True, stop=True).then_inc(s_done, 1)

            def probs_transposed(j, par, g):
                t, n = GROUPS[g]
                divided = count(pe, 3 * j + (1, 1, 1, 2, 2, 3)[g])
                read = count(pe, 3 * j + g // 2 + 1)
                pe.wait_ge(consts_ready, 2)
                if g in (0, 3, 5):
                    pe.wait_ge(p_ready, divided)
                if g >= 2 or has(j, 1, PAIRS):
                    pe.wait_ge(pt_ready[g % 2], read)
                for h in range(2):
                    last = nc.tensor.transpose(T_BANK[g % 2][0:n, h * UW:h * UW + n], P[par][0:n, 2 * g + h, 0:n],
                                               ident[0:n, 0:n])
                last.then_inc(t_done, 1)

            def attend(j, par, g):
                t, n = GROUPS[g]
                half, at = g // 3, t - ZHALF[g // 3][0]
                if g == 0:
                    pe.wait_ge(vp_ready, j + 1)
                if g % 3 == 0 and has(j, 1, PAIRS):
                    pe.wait_ge(z_ready[half], j + 1)
                here = count(pe, 3 * j + g // 2 + 2)
                if g == NG - 1:
                    pe.wait_ge(ld_cols, 16)
                pe.wait_ge(pt_ready[g % 2], here)
                for h in range(2):
                    last = mm(Z_BANK[half][64 * h:64 * h + 64, at:at + n], Vp[par][0:n, g, 64 * h:64 * h + 64],
                              PT[g % 2][0:n, h, 0:n], start=True, stop=True)
                if g % 3 == 2:
                    last.then_inc(z_done[half], 1)

            def output(i, pairs):
                t, n = TILES[i]
                for j in pairs:
                    if j == 0:
                        pe.wait_ge(wo_ready, 1)
                        if i == 0:
                            pe.wait_ge(k_ready, 2 * PAIRS)
                        if i == 2:
                            pe.wait_ge(sm_ready, UNITS * PAIRS)
                        if i == 4:
                            pe.wait_ge(pt_ready[0], 3 * PAIRS + 1)
                    pe.wait_ge(z_ready[0], j + 2)
                    if t + n > ZHALF[0][1]:
                        pe.wait_ge(z_ready[1], j + 2)
                    tok, w = slice(j * TOKENS + t, j * TOKENS + t + n), slice(j * DIM, (j + 1) * DIM)
                    for m, (a, b) in enumerate(((z_hi, wo_hi), (z_hi, wo_lo), (z_lo, wo_hi))):
                        last = mm(O_BANK[i][0:n, 0:DIM], a[:, tok], b[:, w],
                                  start=(j == 0 and m == 0), stop=(j == PAIRS - 1 and m == 2))
                        if j == PAIRS - 1 and m == 2:
                            last.then_inc(o_done, 1)
                        yield

            def step(j, par):
                if has(j, 0, PAIRS - 1):
                    passes = projection(j + 1, 1 - par)
                elif j == PAIRS - 1:
                    passes = (p for i in range(2) for p in output(i, range(PAIRS - 3)))
                else:
                    passes = (p for i, pairs in ((0, range(PAIRS - 3, PAIRS - 1)), (1, range(PAIRS - 3, PAIRS - 1)),
                                                 (2, range(PAIRS - 1))) for p in output(i, pairs))
                for g in range(NG + 1):
                    for _ in range(PASSES_AT[g][0]):
                        next(passes, None)
                    if g < NG and has(j, 1, PAIRS + 1):
                        probs_transposed(j - 1, 1 - par, g)
                    if not has(j, 0, PAIRS):
                        for _ in range(3):
                            next(passes, None)
                    if g >= 1 and has(j, 1, PAIRS + 1):
                        attend(j - 1, 1 - par, g - 1)
                    if g < NG and has(j, 0, PAIRS):
                        scores(j, par, g)
                    for _ in range(PASSES_AT[g][1]):
                        next(passes, None)
                if not has(j, 0, PAIRS - 1):
                    for _ in passes:
                        pass

            steps(pe, step)

            def up(c, f):
                t0, t1, _, i1 = FFN_CHUNKS[c]
                n = c * FT + f
                if f == 0:
                    pe.wait_ge(xn_ready, NT + i1)
                if n >= 3:
                    pe.wait_ge(relu_done, n - 2)
                terms = [(k, b) for k in range(KD) for b in (xn_hi, xn_lo)]
                for m, (k, b) in enumerate(terms):
                    last = mm(U_BANK[n % 3][:, 0:t1 - t0], w1q[:, k * FF + f * 128:k * FF + f * 128 + 128], b[:, k, t0:t1],
                              start=(m == 0), stop=(m == len(terms) - 1))
                last.then_inc(f1_done, 1)

            def down(i):
                t, n = TILES[i]
                pe.wait_ge(ff_ready, FT if i < FFN_CHUNKS[0][3] else 2 * FT)
                if i < 3:
                    pe.wait_ge(h_ready, NT + 3 + i)
                for f in range(FT):
                    for m, a in enumerate((h_hi, h_lo)):
                        last = mm(D_BANK[i][0:n, 0:DIM], a[:, f, t:t + n], w2q[:, f * DIM:(f + 1) * DIM],
                                  start=(f == 0 and m == 0), stop=(f == FT - 1 and m == 1))
                        if f == FT - 1 and m == 1:
                            last.then_inc(f2_done, 1)
                        yield

            def finish(passes):
                for _ in passes:
                    pass

            finish(output(0, range(PAIRS - 1, PAIRS)))
            finish(output(1, range(PAIRS - 1, PAIRS)))
            finish(output(2, range(PAIRS - 1, PAIRS)))
            pe.wait_ge(pt_ready[1], 3 * PAIRS + 1)
            transposes(NT)
            finish(output(3, range(PAIRS)))
            transposes(NT + 1)
            finish(output(4, range(PAIRS)))
            transposes(NT + 2)
            pe.wait_ge(wff_ready, 2)
            for f in range(FT):
                up(0, f)
                if f % 4 == 3:
                    transposes(NT + 3 + f // 4)
            downs = (p for i in range(FFN_CHUNKS[0][3]) for p in down(i))
            for f in range(FT):
                up(1, f)
                for _ in range(7 if f >= 3 else 0):
                    next(downs, None)
            finish(downs)
            for i in range(FFN_CHUNKS[0][3], NT):
                finish(down(i))


def kernel(**inputs):
    import numpy as np
    import concourse.bacc as bacc
    from concourse.bass_utils import run_bass_kernel_spmd

    def two(a, width):
        return np.ascontiguousarray(a.reshape(-1, 128, width).transpose(1, 0, 2))

    g = {k: np.asarray(v) for k, v in inputs.items()}
    p = g["x"].reshape(IMAGES, 3, 6, 16, 6, 16).transpose(0, 2, 4, 1, 3, 5).reshape(IMAGES, SEQ - 1, PATCH_DIM)
    tok = np.zeros((IMAGES, SEQ, PATCH_DIM), p.dtype)
    tok[:, 1:] = p
    xt = tok.reshape(TOKENS, PATCH_DIM).T.reshape(KP, 128, TOKENS)
    wt = g["L0_tok_W"].T.reshape(KP, 128, DIM)
    wq, wk, wvt = (g[f"L0_attn_W_{n}"].reshape(HEADS * HEAD_DIM, DIM).T for n in "QKV")
    wqk = np.stack([a.reshape(KD, 128, PAIRS, 128) for a in (wq, wk)], 3)
    arrays = {
        "xw": np.ascontiguousarray(np.concatenate([xt, wt], 2)),
        "wqk": np.ascontiguousarray(wqk.transpose(1, 2, 0, 3, 4)).reshape(128, PAIRS * KD * 256),
        "wv": two(wvt, FF),
        "wo": two(g["L0_attn_W_O"].transpose(0, 2, 1).reshape(HEADS * HEAD_DIM, DIM), DIM).reshape(128, PAIRS * DIM),
        "w1": two(g["L0_ffn_W1"].T, FF).reshape(128, KD * FF),
        "w2": two(g["L0_ffn_W2"].T, DIM).reshape(128, FT * DIM),
        "bias_cols": np.ascontiguousarray(np.concatenate(
            [g[n].reshape(8, 128).T for n in ("L0_attn_b_Q", "L0_attn_b_K", "L0_attn_b_V", "L0_ffn_b1")], 1)),
        "bias_rows": np.concatenate([g["L0_attn_b_O"], g["L0_ffn_b2"]]).reshape(1, 2 * DIM),
        "tok_bias": g["L0_tok_b"].reshape(1, DIM),
        "cls": g["L0_tok_cls_token"].reshape(1, DIM),
        "pos": np.ascontiguousarray(g["L0_tok_pos_embed"].reshape(SEQ, DIM)),
    }
    nc = bacc.Bacc("TRN2", target_bir_lowering=False, num_devices=1)
    args = [nc.dram_tensor(f"in_{n}", a.shape, mybir.dt.from_np(a.dtype), kind="ExternalInput").ap()
            for n, a in arrays.items()]
    out = nc.dram_tensor("out", (TOKENS, DIM), F32, kind="ExternalOutput").ap()
    vit_block(nc, *args, out)
    r = run_bass_kernel_spmd(nc, [{f"in_{n}": a for n, a in arrays.items()}], core_ids=[0])
    return r.results[0]["out"].reshape(IMAGES, SEQ, DIM)
```

```python
import concourse.bass as bass
from concourse import mybir
from contextlib import ExitStack
from itertools import zip_longest

F32 = mybir.dt.float32
F32R = mybir.dt.float32r
ALU = mybir.AluOpType
ACT = mybir.ActivationFunctionType
AX = mybir.AxisListType

IMAGES, SEQ, DIM = 16, 37, 256
TOKENS = IMAGES * SEQ
PATCH_DIM = 3 * 16 * 16
KP = PATCH_DIM // 128
KD = DIM // 128
HEADS, HEAD_DIM = 16, 64
PAIRS = HEADS // 2
FF = 1024
FT = FF // 128
TILES = [(t, min(128, TOKENS - t)) for t in range(0, TOKENS, 128)]
NT = len(TILES)
PER_GROUP = 128 // SEQ
GROUP = PER_GROUP * SEQ
GROUPS = [(g, min(GROUP, TOKENS - g)) for g in range(0, TOKENS, GROUP)]
NG = len(GROUPS)
UNITS = 2 * NG
UW = GROUP + 1
HALF = TOKENS // 2
ZHALF = [(0, 3 * GROUP), (3 * GROUP, TOKENS)]
FFN_CHUNKS = [(0, 256, 0, 2), (256, TOKENS, 2, NT)]
EARLY = 4
PASSES_AT = [(3, 1), (4, 0), (2, 2), (2, 2), (2, 2), (2, 2), (0, 0)]
KEYS_AT = (4, 5)
SPLIT_AT = (1, 2)
VALUES_BEFORE = 3
VALUES_AT = 1
RELUS = 3
TILE_AFTER = {1: 2, 2: 3, 4: 4}
DOWNS_AT = [[0, 0, 0, 0, 2, 2, 2, 2], [2, 2, 2, 2, 2, 2, 2, 2]]
EPS = 1e-5
SCALE = float(HEAD_DIM) ** -0.5
HIDDEN_KEY = -1e5 / SCALE
OTHER_IMAGE = -1e30


def vit_block(nc, xw, wqk, wv, wo, w1, w2, bias_cols, bias_rows, tok_bias, cls, pos, out):
    with ExitStack() as ctx:
        def sb(name, shape, dt=F32):
            return ctx.enter_context(nc.sbuf_tensor(name, shape, dt))

        def overlay(*specs):
            def size(spec):
                n = 1
                for d in spec[1][1:]:
                    n *= d
                return n
            held = max(range(len(specs)), key=lambda i: size(specs[i]))
            tensors = {}
            for i, spec in enumerate(specs):
                if i != held:
                    with nc.sbuf_tensor(*spec) as tensors[i]:
                        pass
            tensors[held] = sb(*specs[held])
            return [tensors[i] for i in range(len(specs))]

        def sem(name):
            return ctx.enter_context(nc.semaphore(name))

        XW = [128, KP, TOKENS + DIM]
        xw_sb, attn = overlay(("xw_sb", XW, F32), ("attn", [128, 3 * UNITS * UW], F32))
        xw_hi, z_hi = overlay(("xw_hi", XW, F32R), ("z_hi", [128, PAIRS * TOKENS], F32R))
        xw_lo, V, h_lo = overlay(("xw_lo", XW, F32R), ("V", [128, NG, FF], F32), ("h_lo", [128, FT, TOKENS], F32R))
        wqk_sb, h_hi = overlay(("wqk_sb", [128, (PAIRS + 1) * KD * 256], F32), ("h_hi", [128, FT, TOKENS], F32R))
        wv_sb = sb("wv_sb", [128, KD, FF])
        wv_split, z_lo = overlay(("wv_split", [128, 2 * KD, FF], F32R), ("z_lo", [128, PAIRS * TOKENS], F32R))
        wv_hi, wv_lo = wv_split[:, 0:KD, :], wv_split[:, KD:2 * KD, :]
        wo_sb = sb("wo_sb", [128, PAIRS * DIM])
        w1_sb, wo_hi = overlay(("w1_sb", [128, KD * FF], F32), ("wo_hi", [128, PAIRS * DIM], F32R))
        w2_sb, wo_lo = overlay(("w2_sb", [128, FT * DIM], F32), ("wo_lo", [128, PAIRS * DIM], F32R))
        cols = sb("cols", [128, 4 * 8])
        rows = sb("rows", [128, 2 * DIM])
        pos_sb, xn = overlay(("pos_sb", [SEQ, DIM], F32), ("xn", [128, NT, DIM], F32))
        first_sb = sb("first_sb", [SEQ, DIM])
        ident = sb("ident", [128, 128])
        first_hi, first_lo = sb("first_hi", [SEQ, DIM], F32R), sb("first_lo", [SEQ, DIM], F32R)
        onehot, pt = overlay(("onehot", [SEQ, TOKENS], F32R), ("pt", [GROUP, 4 * UW], F32))
        mask = sb("mask", [GROUP, UW])
        ones = sb("ones", [128, 128])
        power = sb("power", [128, 1])
        wqk_hi = [sb(f"wqk_hi{n}", [128, KD * 256], F32R) for n in range(2)]
        wqk_lo = [sb(f"wqk_lo{n}", [128, KD * 256], F32R) for n in range(2)]
        w1q, w2q = sb("w1q", [128, KD * FF], F32R), sb("w2q", [128, FT * DIM], F32R)
        below = wv_sb[:, :, :].rearrange("p k n -> p (k n)")
        absum = sb("absum", [128, 2])
        gate = sb("gate", [128, 4])
        h0 = sb("h0", [128, NT, DIM])
        h1 = sb("h1", [128, NT, DIM])
        stat = sb("stat", [128, NT, 6])
        mv = sb("mv", [128, NT, 2])
        ve = sb("ve", [128, NT])
        rs0, rs1 = sb("rs0", [128, NT]), sb("rs1", [128, NT])
        rt0, rt1 = sb("rt0", [128, NT]), sb("rt1", [128, NT])
        XC = GROUP * NG
        xn_hi, xn_lo = sb("xn_hi", [128, KD, XC], F32R), sb("xn_lo", [128, KD, XC], F32R)
        V = V[0:GROUP, :, :]
        Vp = [sb(f"Vp{n}", [GROUP, NG, 128]) for n in range(2)]
        HR = max(b - a for a, b, _, _ in FFN_CHUNKS)
        qk, late = overlay(("qk", [128, 4 * TOKENS], F32), ("late", [128, RELUS * HR + NT * DIM], F32))
        QT = [qk[:, n * TOKENS:(n + 1) * TOKENS] for n in (0, 1)]
        KT = [qk[:, n * TOKENS:(n + 1) * TOKENS] for n in (2, 3)]
        hr = [late[:, n * HR:(n + 1) * HR] for n in range(RELUS)]
        y = late[:, RELUS * HR:].rearrange("p (i n) -> p i n", n=DIM)
        by_unit = attn[0:GROUP, :].rearrange("p (a u c) -> p a u c", a=3, c=UW)
        P = [by_unit[:, 0], by_unit[:, 1]]
        SM = by_unit[:, 2]
        nmax = sb("nmax", [GROUP, UNITS])
        rsum = sb("rsum", [GROUP, UNITS])
        rinv = sb("rinv", [GROUP, UNITS])
        PT = [pt[:, n * 2 * UW:(n + 1) * 2 * UW].rearrange("p (h q) -> p h q", h=2) for n in range(2)]

        B = [ctx.enter_context(nc.psum_tensor(f"bank{n}", [128, 512], F32)) for n in range(8)]
        S_BANK, T_BANK, Z_BANK, J_BANK = B[0:2], B[2:4], B[4:6], B[6:8]
        XT_BANK = [B[6:8], [B[3], B[5]]]
        O_BANK = [B[6], B[7], B[0], B[1], B[2]]
        U_BANK = [B[4], B[6], B[7]]
        D_BANK = [B[0], B[1], B[2], B[3], B[5]]

        ld_xw = [sem(f"ld_xw{k}") for k in range(KP)]
        ld_small, ld_cols, ld_rows = sem("ld_small"), sem("ld_cols"), sem("ld_rows")
        ld_wqk01 = sem("ld_wqk01")
        ld_wv = [sem("ld_wv0"), sem("ld_wv1")]
        ld_wqk, ld_wo, ld_w1, ld_w2 = (sem(f"ld_{n}") for n in ("wqk", "wo", "w1", "w2"))
        filled = sem("filled")
        consts_ready = sem("consts_ready")
        zeros_ready = sem("zeros_ready")
        add_ready = sem("add_ready")
        xwh_done, xw_ready = sem("xwh_done"), sem("xw_ready")
        fh_done, first_ready = sem("fh_done"), sem("first_ready")
        woh_done, wo_ready = sem("woh_done"), sem("wo_ready")
        emb_done = sem("emb_done")
        h_ready = sem("h_ready")
        stat_done, mv_done, ve_ready = sem("stat_done"), sem("mv_done"), sem("ve_ready")
        pow_done, nt_a, rstd_ready = sem("pow_done"), sem("nt_a"), sem("rstd_ready")
        xn_done = sem("xn_done")
        xt_done = sem("xt_done")
        xh_done, xn_ready = sem("xh_done"), sem("xn_ready")
        wvh_done, wv_ready = sem("wvh_done"), sem("wv_ready")
        wqh_done, wq_ready = sem("wqh_done"), sem("wq_ready")
        abs_done, total_done, gam_done, gate_done, gate_ready = (
            sem(n) for n in ("abs_done", "total_done", "gam_done", "gate_done", "gate_ready"))
        below_done, wff_ready = sem("below_done"), sem("wff_ready")
        v_done = sem("v_done")
        v_ready = sem("v_ready")
        vp_ready = sem("vp_ready")
        proj_done = sem("proj_done")
        q_ready, k_ready = sem("q_ready"), sem("k_ready")
        s_done, sm_ready, exp_done = sem("s_done"), sem("sm_ready"), sem("exp_done")
        inv_ready, p_ready = sem("inv_ready"), sem("p_ready")
        t_done = sem("t_done")
        pt_ready = [sem("pt_even_ready"), sem("pt_odd_ready")]
        z_done, z_ready = [sem("z0_done"), sem("z1_done")], [sem("z0_ready"), sem("z1_ready")]
        zh_done = [sem("zh0_done"), sem("zh1_done")]
        hb0_ready, hb1_ready = sem("hb0_ready"), sem("hb1_ready")
        o_done = sem("o_done")
        f1_done, relu_done = sem("f1_done"), sem("relu_done")
        hh_done, ff_ready = [sem("hh0_done"), sem("hh1_done")], [sem("ff0_ready"), sem("ff1_ready")]
        f2_done, y_ready, stored = sem("f2_done"), sem("y_ready"), sem("stored")

        block = ctx.enter_context(nc.Block())

        def cols_of(group_units, j):
            return cols[:, bass.ds(group_units * 8 + j, 1)]

        def steps(eng, step):
            step(0, 0)
            with eng.Fori(0, PAIRS // 2 - 1) as twice:
                step(twice * 2 + 1, 1)
                step(twice * 2 + 2, 0)
            step(PAIRS - 1, 1)
            step(PAIRS, 0)

        def count(eng, value):
            if not isinstance(value, int):
                eng.lower_val(value)
            return value

        def has(j, lo, hi):
            return lo <= j < hi if isinstance(j, int) else True

        def first_step(j):
            return isinstance(j, int) and j == 0

        def last_step(j):
            return isinstance(j, int) and j == PAIRS

        @block.sync
        def _(sp):
            for k in range(KP):
                if k == KP - 1:
                    sp.dma_start(pos_sb[:, :], pos).then_inc(ld_small, 16)
                    sp.dma_start(first_sb[0:1, :], cls).then_inc(ld_small, 16)
                    sp.dma_start(first_sb[1:SEQ, :], tok_bias.broadcast_to([SEQ - 1, DIM])).then_inc(ld_small, 16)
                    sp.dma_start(wv_sb[:, 0, :], wv[:, 0, :]).then_inc(ld_wv[0], 16)
                sp.dma_start(xw_sb[:, k, :], xw[k]).then_inc(ld_xw[k], 16)
            sp.dma_start(wv_sb[:, 1, :], wv[:, 1, :]).then_inc(ld_wv[1], 16)
            sp.dma_start(cols[:, :], bias_cols).then_inc(ld_cols, 16)
            sp.dma_start(rows[:, :], bias_rows.broadcast_to([128, 2 * DIM])).then_inc(ld_rows, 16)
            first = 2 * KD * 256
            sp.dma_start(wqk_sb[:, 0:first], wqk[:, 0:first]).then_inc(ld_wqk01, 16)
            sp.dma_start(w1_sb[:, :], w1).then_inc(ld_w1, 16)
            sp.dma_start(w2_sb[:, :], w2).then_inc(ld_w2, 16)
            sp.dma_start(wqk_sb[:, first:PAIRS * KD * 256], wqk[:, first:]).then_inc(ld_wqk, 16)
            sp.dma_start(wo_sb[:, :], wo).then_inc(ld_wo, 16)

            def step(j, par):
                if has(j, 0, PAIRS):
                    read, copied = count(sp, j), count(sp, 16 * j)
                    sp.wait_ge(v_ready, 2 * NG)
                    if has(j, 1, PAIRS):
                        sp.wait_ge(z_ready[1], read)
                        sp.wait_ge(vp_ready, copied)
                    sp.dma_start(Vp[par][:, :, :], V[:, :, bass.ds(j * 128, 128)]).then_inc(vp_ready, 16)

            steps(sp, step)

            for i, (t, n) in enumerate(TILES):
                sp.wait_ge(y_ready, i + 1)
                sp.dma_start(out[t:t + n, :], y[0:n, i, :]).then_inc(stored, 16)
            sp.wait_ge(stored, 16 * NT)

        @block.gpsimd
        def _(pool):
            pool.memset(onehot[:, :].bitcast(F32), 0.0).then_inc(filled, 1)
            pool.memset(ident[:, :], 0.0).then_inc(filled, 1)
            pool.memset(mask[:, :], 0.0).then_inc(filled, 1)
            pool.memset(power[:, :], -0.5).then_inc(filled, 1)
            pool.wait_ge(filled, 4)
            pool.affine_select(out=onehot[:, :], in_=onehot[:, :].bitcast(F32), compare_op=ALU.not_equal, fill=1.0, base=0,
                               pattern=[[0, IMAGES], [-1, SEQ]], channel_multiplier=1).then_inc(consts_ready, 1)
            pool.affine_select(out=ident[:, :], in_=ident[:, :], compare_op=ALU.not_equal, fill=1.0, base=0,
                               pattern=[[-1, 128]], channel_multiplier=1).then_inc(consts_ready, 1)
            mk = mask[:, 0:GROUP]
            pool.affine_select(out=mk, in_=mk, compare_op=ALU.is_ge, fill=HIDDEN_KEY, base=0,
                               pattern=[[-1, GROUP]], channel_multiplier=1).then_inc(filled, 1)
            pool.wait_ge(filled, 5)
            pool.affine_select(out=mk, in_=mk, compare_op=ALU.is_ge, fill=OTHER_IMAGE, base=0,
                               pattern=[[-SEQ, PER_GROUP], [0, SEQ]], channel_multiplier=1).then_inc(filled, 1)
            pool.wait_ge(filled, 6)
            pool.affine_select(out=mk, in_=mk, compare_op=ALU.is_ge, fill=OTHER_IMAGE, base=SEQ - 1,
                               pattern=[[SEQ, PER_GROUP], [0, SEQ]], channel_multiplier=-1).then_inc(consts_ready, 1)

            def inverse_root(i, rs):
                pool.wait_ge(ve_ready, i + 1)
                t = i % NT
                n = TILES[t][1]
                pool.tensor_tensor(rs[0:n, t:t + 1], ve[0:n, t:t + 1], power[0:n, :], ALU.pow).then_inc(pow_done, 1)

            for i in range(NT):
                inverse_root(i, rs0)

            pool.wait_ge(ld_rows, 16)
            for i, (t, n) in enumerate(TILES):
                pool.wait_ge(h_ready, i + 1)
                pool.wait_ge(xn_done, i + 1)
                pool.tensor_tensor(h0[0:n, i, :], h0[0:n, i, :], rows[0:n, 0:DIM], ALU.add).then_inc(hb0_ready, 1)

            pool.wait_ge(wff_ready, 2)
            pool.wait_ge(woh_done, 1)
            pool.tensor_tensor(wo_lo[:, :], wo_sb[:, :], wo_hi[:, :].bitcast(F32),
                               ALU.subtract).then_inc(wo_ready, 1)

            def step(j, par):
                if has(j, 0, PAIRS):
                    for half, units, n in ((0, slice(0, 6), GROUP), (1, slice(6, 10), GROUP), (1, slice(10, 12), SEQ)):
                        pool.wait_ge(inv_ready, 2 * j + half + 1)
                        pool.wait_ge(exp_done, 12 * j + units.stop)
                        p = P[par][0:n, units, 0:n]
                        pool.tensor_tensor(p, p, rinv[0:n, units].unsqueeze(2).broadcast_to(list(p.shape)),
                                           ALU.mult).then_inc(p_ready, 1)

            steps(pool, step)

            for i in range(NT):
                inverse_root(NT + i, rs1)
            t0, t1, _, _ = FFN_CHUNKS[0]
            for f in range(FT):
                pool.wait_ge(hh_done[0], f + 1)
                pool.tensor_tensor(h_lo[:, f, t0:t1], hr[f % RELUS][:, 0:t1 - t0], h_hi[:, f, t0:t1].bitcast(F32),
                                   ALU.subtract).then_inc(ff_ready[0], 1)
            for i, (t, n) in enumerate(TILES):
                pool.wait_ge(h_ready, NT + i + 1)
                pool.wait_ge(xn_done, NT + i + 1)
                pool.tensor_tensor(h1[0:n, i, :], h1[0:n, i, :], rows[0:n, DIM:2 * DIM], ALU.add).then_inc(hb1_ready, 1)

        def transposed_hi(act, i):
            t, n = TILES[i % NT]
            act.wait_ge(xt_done, i + 1)
            bank = XT_BANK[i // NT][i % 2]
            act.activation(xn_hi[:, :, t:t + n], bank[:, 0:2 * 128].rearrange("p (k t) -> p k t", k=2)[:, :, 0:n],
                           ACT.Copy, scale=-0.5).then_inc(xh_done, 1)

        def relu(act, c, f):
            t0, t1, _, _ = FFN_CHUNKS[c]
            n = c * FT + f
            act.wait_ge(f1_done, n + 1)
            if n >= RELUS:
                last = n - RELUS
                act.wait_ge(ff_ready[last // FT], last % FT + 1)
            act.activation(hr[n % RELUS][:, 0:t1 - t0], U_BANK[n % 3][:, 0:t1 - t0], ACT.Relu,
                           bias=cols[:, 24 + f:25 + f]).then_inc(relu_done, 1)

        def hidden_hi(act, f):
            t0, t1, _, _ = FFN_CHUNKS[0]
            act.wait_ge(relu_done, f + 1)
            act.activation(h_hi[:, f, t0:t1], hr[f % RELUS][:, 0:t1 - t0], ACT.Copy).then_inc(hh_done[0], 1)

        @block.scalar
        def _(act):
            def values_weights_hi(k):
                act.wait_ge(ld_wv[k], 16)
                act.activation(wv_hi[:, k, :], wv_sb[:, k, :], ACT.Copy).then_inc(wvh_done, 1)

            for k in range(KP):
                if k == KP - 1:
                    values_weights_hi(0)
                act.wait_ge(ld_xw[k], 16)
                act.activation(xw_hi[:, k, :], xw_sb[:, k, :], ACT.Copy).then_inc(xwh_done, 1)
            values_weights_hi(1)
            for i, (t, n) in enumerate(TILES):
                act.wait_ge(stat_done, i + 1)
                act.activation(h0[0:n, i, :], B[i][0:n, 0:DIM], ACT.Copy).then_inc(h_ready, 1)
                if 2 <= i < 4:
                    transposed_hi(act, i - 2)
            def sum_of_magnitudes(m):
                act.wait_ge((ld_w1, ld_w2)[m], 16)
                if m:
                    act.wait_ge(abs_done, m)
                else:
                    act.wait_ge(wv_ready, KD)
                act.activation(below, (w1_sb, w2_sb)[m][:, :], ACT.Abs,
                               accum_out=absum[:, m:m + 1]).then_inc(abs_done, 1)

            def values_out(g):
                for half in range(2):
                    act.wait_ge(v_done, 2 * g + half + 1)
                    act.activation(V[:, g, half * 512:half * 512 + 512], B[(2 * g + half) % 4][0:GROUP, :],
                                   ACT.Copy).then_inc(v_ready, 1)

            for m in range(2):
                sum_of_magnitudes(m)
                transposed_hi(act, 2 + m)
                values_out(m)
            transposed_hi(act, 4)
            for g in range(2, NG - 2):
                values_out(g)

            def queries(j, par, c):
                n = count(act, 4 * j + c + 1)
                act.wait_ge(ld_cols, 16)
                act.wait_ge(proj_done, n)
                act.activation(QT[par][:, c * HALF:(c + 1) * HALF], J_BANK[c][:, 0:HALF], ACT.Identity,
                               bias=cols_of(0, j)).then_inc(q_ready, 1)

            queries(0, 0, 0)
            queries(0, 0, 1)
            act.wait_ge(wff_ready, 1)
            act.wait_ge(ld_wo, 16)
            act.activation(wo_hi[:, :], wo_sb[:, :], ACT.Copy).then_inc(woh_done, 1)
            values_out(NG - 2)

            def attended_hi(j, half):
                a, b = ZHALF[half]
                n = count(act, j + 1)
                act.wait_ge(ld_cols, 16)
                act.wait_ge(z_done[half], n)
                act.activation(z_hi[:, bass.ds(j * TOKENS + a, b - a)], Z_BANK[half][:, 0:b - a], ACT.Identity,
                               bias=cols_of(2, j)).then_inc(zh_done[half], 1)

            def odd_transposed(j, g):
                n = GROUPS[g][1]
                act.wait_ge(t_done, 6 * j + g + 1)
                act.activation(PT[1][0:n, :, 0:n],
                               T_BANK[1][0:n, 0:2 * UW].rearrange("p (h q) -> p h q", h=2)[:, :, 0:n],
                               ACT.Copy).then_inc(pt_ready[1], 1)

            def step(j, par):
                for g, (t, n) in enumerate(GROUPS):
                    if g == 1 and has(j, 0, PAIRS - 1):
                        queries(j + 1, 1 - par, 0)
                    if g == 4 and has(j, 1, PAIRS + 1) and not last_step(j):
                        attended_hi(j - 1, 0)
                    if has(j, 0, PAIRS):
                        for h in range(2):
                            u = 2 * g + h
                            if h == 1 and g % 2 == 0 and has(j, 1, PAIRS + 1):
                                odd_transposed(j - 1, g + 1)
                            act.wait_ge(sm_ready, 12 * j + u + 1)
                            act.activation(P[par][0:n, u, 0:n], SM[0:n, u, 0:n], ACT.Exp, bias=nmax[0:n, u:u + 1],
                                           scale=-1.0, accum_out=rsum[0:n, u:u + 1]).then_inc(exp_done, 1)

                    if g == 2 and has(j, 0, PAIRS - 1):
                        queries(j + 1, 1 - par, 1)
                    if first_step(j) and g == VALUES_AT:
                        values_out(NG - 1)
                    if last_step(j) and g % 2 == 0:
                        if g == 4:
                            attended_hi(j - 1, 0)
                        odd_transposed(j - 1, g + 1)
                if has(j, 1, PAIRS + 1):
                    attended_hi(j - 1, 1)

            steps(act, step)

            for i in range(2):
                transposed_hi(act, NT + i)
            for f in range(FT):
                relu(act, 0, f)
                if f >= 1:
                    hidden_hi(act, f - 1)
                if f in TILE_AFTER:
                    transposed_hi(act, NT + TILE_AFTER[f])
            hidden_hi(act, FT - 1)
            for f in range(FT):
                relu(act, 1, f)

        def hidden(dve):
            t0, t1, _, _ = FFN_CHUNKS[1]
            for f in range(FT + 1):
                if f < FT:
                    dve.wait_ge(relu_done, FT + f + 1)
                    dve.tensor_copy(h_hi[:, f, t0:t1], hr[(FT + f) % RELUS][:, 0:t1 - t0]).then_inc(hh_done[1], 1)
                if f >= 1:
                    dve.wait_ge(hh_done[1], f)
                    dve.tensor_tensor(h_lo[:, f - 1, t0:t1], hr[(FT + f - 1) % RELUS][:, 0:t1 - t0],
                                      h_hi[:, f - 1, t0:t1].bitcast(F32), ALU.subtract).then_inc(ff_ready[1], 1)

        @block.vector
        def _(dve):
            dve.memset(ones[:, :], 1.0).then_inc(zeros_ready, 1)
            dve.memset(wqk_sb[:, PAIRS * KD * 256:], 0.0).then_inc(zeros_ready, 1)
            for k in range(KD):
                dve.memset(xn_hi[:, k, TOKENS:].bitcast(F32), 0.0).then_inc(zeros_ready, 1)
                dve.memset(xn_lo[:, k, TOKENS:].bitcast(F32), 0.0).then_inc(zeros_ready, 1)
            dve.memset(rsum[:, :], 1.0).then_inc(zeros_ready, 1)
            for n, free in enumerate((*pt_ready, *z_ready)):
                dve.memset(rinv[:, n:n + 1], 1.0).then_inc(free, 1)
            def values_weights_lo(k):
                dve.wait_ge(wvh_done, k + 1)
                dve.tensor_tensor(wv_lo[:, k, :], wv_sb[:, k, :], wv_hi[:, k, :].bitcast(F32),
                                  ALU.subtract).then_inc(wv_ready, 1)

            for k in range(KP):
                if k == KP - 1:
                    dve.wait_ge(ld_small, 48)
                    dve.tensor_tensor(first_sb[:, :], first_sb[:, :], pos_sb[:, :], ALU.add).then_inc(add_ready, 1)
                    dve.wait_ge(add_ready, 1)
                    dve.tensor_copy(first_hi[:, :], first_sb[:, :]).then_inc(fh_done, 1)
                    dve.wait_ge(fh_done, 1)
                    dve.tensor_tensor(first_lo[:, :], first_sb[:, :], first_hi[:, :].bitcast(F32),
                                      ALU.subtract).then_inc(first_ready, 1)
                    values_weights_lo(0)
                dve.wait_ge(xwh_done, k + 1)
                dve.tensor_tensor(xw_lo[:, k, :], xw_sb[:, k, :], xw_hi[:, k, :].bitcast(F32),
                                  ALU.subtract).then_inc(xw_ready, 1)
            values_weights_lo(1)

            def variance(i, src):
                t = i % NT
                n = TILES[t][1]
                dve.wait_ge(emb_done if i < NT else h_ready, i + 1)
                dve.bn_stats(stat[0:n, t, :], src).then_inc(stat_done, 1)
                yield
                dve.wait_ge(stat_done, i + 1)
                dve.bn_aggr(mv[0:n, t, :], stat[0:n, t, :]).then_inc(mv_done, 1)
                yield
                dve.wait_ge(mv_done, i + 1)
                dve.tensor_scalar(ve[0:n, t:t + 1], mv[0:n, t, 1:2], EPS, None, ALU.add).then_inc(ve_ready, 1)
                yield

            def normalise(i, h, rs, rt):
                t = i % NT
                n = TILES[t][1]
                r, w, v = rs[0:n, t:t + 1], rt[0:n, t:t + 1], ve[0:n, t:t + 1]
                dve.wait_ge(pow_done, i + 1)
                dve.scalar_tensor_tensor(w, r, r, v, ALU.mult, ALU.mult).then_inc(nt_a, 1)
                yield
                dve.wait_ge(nt_a, i + 1)
                dve.scalar_tensor_tensor(w, w, -3.0, r, ALU.add, ALU.mult).then_inc(rstd_ready, 1)
                yield
                dve.wait_ge(rstd_ready, i + 1)
                if i < NT:
                    dve.wait_ge(h_ready, i + 1)
                else:
                    dve.wait_ge(xt_done, i - NT + 1)
                dve.tensor_scalar(xn[0:n, t, :], h[0:n, t, :], mv[0:n, t, 0:1], w,
                                  ALU.subtract, ALU.mult).then_inc(xn_done, 1)
                yield

            def lone(part, *args):
                part(*args)
                yield

            def together(*chains):
                for parts in zip_longest(*chains):
                    pass

            def transposed_lo(i):
                t, n = TILES[i % NT]
                dve.wait_ge(xh_done, i + 1)
                src = XT_BANK[i // NT][i % 2][:, 0:2 * 128].rearrange("p (k t) -> p k t", k=2)[:, :, 0:n]
                dve.scalar_tensor_tensor(xn_lo[:, :, t:t + n], src, -0.5, xn_hi[:, :, t:t + n].bitcast(F32),
                                         ALU.mult, ALU.subtract).then_inc(xn_ready, 1)

            def split_pair(j, par):
                src = wqk_sb[:, bass.ds(j * (KD * 256), KD * 256)]
                dve.tensor_copy(wqk_hi[par][:, :], src).then_inc(wqh_done, 1)
                yield
                dve.wait_ge(wqh_done, j + 1)
                dve.tensor_tensor(wqk_lo[par][:, :], src, wqk_hi[par][:, :].bitcast(F32),
                                  ALU.subtract).then_inc(wq_ready, 1)
                yield

            for i in range(NT + 1):
                together(*([variance(i, B[i][0:TILES[i][1], 0:DIM])] if i < NT else []),
                         *([normalise(i - 1, h0, rs0, rt0)] if i else []))
                if 2 <= i < NT:
                    transposed_lo(i - 2)

            def ternary(m):
                src, dst = ((w1_sb, w1q), (w2_sb, w2q))[m]
                if m == 0:
                    dve.wait_ge(abs_done, 2)
                else:
                    dve.wait_ge(wff_ready, 1)
                dve.tensor_scalar(below, src[:, :], gate[:, 2 + m:3 + m], None, ALU.is_lt).then_inc(below_done, 1)
                yield
                dve.wait_ge(below_done, m + 1)
                dve.scalar_tensor_tensor(dst[:, :], src[:, :], gate[:, m:m + 1], below,
                                         ALU.is_gt, ALU.subtract).then_inc(wff_ready, 1)
                yield

            dve.wait_ge(ld_wqk01, 16)
            together(split_pair(0, 0), split_pair(1, 1))
            transposed_lo(3)
            dve.wait_ge(total_done, 1)
            dve.tensor_scalar(gate[:, 0:2], Z_BANK[0][:, 0:2], 1.0 / (DIM * FF), EPS,
                              ALU.mult, ALU.add).then_inc(gam_done, 1)
            dve.wait_ge(gam_done, 1)
            dve.tensor_scalar(gate[:, 2:4], gate[:, 0:2], -0.5, None, ALU.mult).then_inc(gate_done, 1)
            dve.wait_ge(gate_done, 1)
            dve.tensor_scalar(gate[:, 0:2], gate[:, 0:2], 0.5, None, ALU.mult).then_inc(gate_ready, 1)
            dve.wait_ge(gate_ready, 1)
            together(ternary(0), lone(transposed_lo, 4))
            together(ternary(1))

            def keys(j, par, c):
                dve.wait_ge(proj_done, 4 * j + c + 3)
                if first_step(j) and c == 0:
                    dve.wait_ge(ld_cols, 16)
                dve.tensor_scalar(KT[par][:, c * HALF:(c + 1) * HALF], J_BANK[c][:, 0:HALF],
                                  cols_of(1, j), None, ALU.add).then_inc(k_ready, 1)

            keys(0, 0, 0)
            keys(0, 0, 1)

            def residual(i):
                t, n = TILES[i]
                dve.wait_ge(o_done, i + 1)
                dve.wait_ge(hb0_ready, i + 1)
                dve.tensor_tensor(h1[0:n, i, :], O_BANK[i][0:n, 0:DIM], h0[0:n, i, :], ALU.add).then_inc(h_ready, 1)
                yield

            def inverse_sums(j, half):
                u = slice(6 * half, 6 * half + 6)
                dve.wait_ge(exp_done, 12 * j + 6 * half + 6)
                if has(j, 1, PAIRS):
                    dve.wait_ge(p_ready, 3 * j - 2 + 2 * half)
                dve.reciprocal(rinv[:, u], rsum[:, u]).then_inc(inv_ready, 1)

            def masked_scores(j, g):
                t, n = GROUPS[g]
                for h in range(2):
                    u = 2 * g + h
                    if has(j, 1, PAIRS):
                        dve.wait_ge(exp_done, 12 * (j - 1) + u + 1)
                    n_done = count(dve, 12 * j + u + 1)
                    dve.wait_ge(consts_ready, 3)
                    dve.wait_ge(s_done, n_done)
                    dve.tensor_tensor_reduce(
                        out=SM[0:n, u, 0:n], in0=S_BANK[h][0:n, 0:n], in1=mask[0:n, 0:n], scale=-SCALE,
                        scalar=1e38, op0=ALU.add, op1=ALU.min, accum_out=nmax[0:n, u:u + 1],
                    ).then_inc(sm_ready, 1)

            def even_transposed(j, g):
                n = GROUPS[g][1]
                dve.wait_ge(t_done, 6 * j + g + 1)
                dve.tensor_copy(PT[0][0:n, :, 0:n],
                                T_BANK[0][0:n, 0:2 * UW].rearrange("p (h q) -> p h q", h=2)[:, :, 0:n]
                                ).then_inc(pt_ready[0], 1)

            def step(j, par):
                split = iter(())
                for g in range(NG):
                    if g in (2, 4) and has(j, 1, PAIRS + 1):
                        even_transposed(j - 1, g)
                    if has(j, 0, PAIRS):
                        masked_scores(j, g)
                    if g == SPLIT_AT[0] and has(j, 0, PAIRS - 1):
                        dve.wait_ge(proj_done, 4 * (j + 1))
                        if has(j, 0, PAIRS - 2):
                            if first_step(j):
                                dve.wait_ge(ld_wqk, 16)
                            split = split_pair(j + 2, par)
                    if g in SPLIT_AT:
                        next(split, None)
                    if g in KEYS_AT and has(j, 0, PAIRS - 1):
                        keys(j + 1, 1 - par, KEYS_AT.index(g))
                    if g == 0 and par == 0 and has(j, 2, PAIRS + 1):
                        attended_lo(j - 2, 1)
                    if g == 3 and has(j, 0, PAIRS):
                        inverse_sums(j, 0)
                    if last_step(j) and g == 4:
                        attended_lo(j - 1, 0)
                if has(j, 1, PAIRS + 1) and not last_step(j):
                    attended_lo(j - 1, 0)
                if has(j, 0, PAIRS):
                    inverse_sums(j, 1)
                if has(j, 0, PAIRS):
                    even_transposed(j, 0)
                if last_step(j):
                    together(residual(0))
                if par == 0 and has(j, 1, PAIRS + 1):
                    attended_lo(j - 1, 1)

            def attended_lo(j, half):
                a, b = ZHALF[half]
                at = bass.ds(j * TOKENS + a, b - a)
                n = count(dve, j + 1)
                dve.wait_ge(ld_cols, 16)
                dve.wait_ge(zh_done[half], n)
                dve.scalar_tensor_tensor(z_lo[:, at], Z_BANK[half][:, 0:b - a], cols_of(2, j), z_hi[:, at].bitcast(F32),
                                         ALU.add, ALU.subtract).then_inc(z_ready[half], 1)

            steps(dve, step)

            def variance1(i):
                return variance(NT + i, h1[0:TILES[i][1], i, :])

            def normalise1(i):
                return normalise(NT + i, h1, rs1, rt1)

            together(variance1(0), residual(1))
            together(variance1(1))
            together(normalise1(0))
            together(normalise1(1))
            together(residual(2))
            together(variance1(2), residual(3))
            transposed_lo(NT)
            transposed_lo(NT + 1)
            together(variance1(3), normalise1(2))
            together(residual(4))
            together(variance1(4), normalise1(3))
            together(normalise1(4))
            for i in range(2, NT):
                transposed_lo(NT + i)
            hidden(dve)
            for i, (t, n) in enumerate(TILES):
                dve.wait_ge(f2_done, i + 1)
                dve.wait_ge(hb1_ready, i + 1)
                dve.tensor_tensor(y[0:n, i, :], D_BANK[i][0:n, 0:DIM], h1[0:n, i, :], ALU.add).then_inc(y_ready, 1)

        @block.tensor
        def _(pe):
            mm = nc.tensor.matmul

            def finish(passes):
                for _ in passes:
                    pass

            def embed(i, k, parts):
                t, n = TILES[i]
                for m in parts:
                    a, b = ((xw_hi, xw_hi), (xw_hi, xw_lo), (xw_lo, xw_hi))[m]
                    mm(B[i][0:n, 0:DIM], a[:, k, t:t + n], b[:, k, TOKENS:], start=(k == 0 and m == 0), stop=False)

            def transposes(i):
                t, n = TILES[i % NT]
                pe.wait_ge(xn_done, i + 1)
                if i % NT >= 2:
                    pe.wait_ge(xn_ready, i - 1)
                bank = XT_BANK[i // NT][i % 2]
                for k in range(KD):
                    last = nc.tensor.transpose(bank[:, k * 128:k * 128 + n], xn[0:n, i % NT, k * 128:k * 128 + 128],
                                               ident[0:n, 0:n])
                last.then_inc(xt_done, 1)

            def values(g):
                for half in range(2):
                    if 2 * g + half >= 4:
                        pe.wait_ge(v_ready, 2 * g + half - 3)
                    c = slice(half * 512, half * 512 + 512)
                    terms = [(k, a, b) for k in range(KD) for a, b in ((xn_hi, wv_hi), (xn_hi, wv_lo), (xn_lo, wv_hi))]
                    for m, (k, a, b) in enumerate(terms):
                        last = mm(B[(2 * g + half) % 4][0:GROUP, :], a[:, k, g * GROUP:(g + 1) * GROUP], b[:, k, c],
                                  start=(m == 0), stop=(m == len(terms) - 1))
                        if m == len(terms) - 1:
                            last.then_inc(v_done, 1)
                        yield

            for k in range(EARLY):
                for parts in ((0,), (1, 2)):
                    pe.wait_ge((xw_ready if parts[0] else xwh_done), k + 1)
                    for i in range(NT):
                        embed(i, k, parts)
            for i, (t, n) in enumerate(TILES):
                for k in range(EARLY, KP):
                    if i == 0:
                        pe.wait_ge(xw_ready, k + 1)
                    embed(i, k, (0, 1, 2))
                if i == 0:
                    pe.wait_ge(first_ready, 1)
                    pe.wait_ge(consts_ready, 2)
                mm(B[i][0:n, 0:DIM], onehot[:, t:t + n], first_hi[:, :], start=False, stop=False)
                mm(B[i][0:n, 0:DIM], onehot[:, t:t + n], first_lo[:, :], start=False, stop=True).then_inc(emb_done, 1)
                if i >= 3:
                    transposes(i - 3)
            pe.wait_ge(zeros_ready, 7)
            pe.wait_ge(wv_ready, KD)
            for g in range(NG - 2):
                pe.wait_ge(xn_ready, min(NT, g + 1))
                if g < 2:
                    pe.wait_ge(h_ready, 2 * g + 2)
                passes = values(g)
                if g == 2:
                    for _ in range(6):
                        next(passes)
                    pe.wait_ge(abs_done, 2)
                    pe.wait_ge(h_ready, NT)
                    mm(Z_BANK[0][:, 0:2], ones[:, :], absum[:, :], start=True, stop=True).then_inc(total_done, 1)
                finish(passes)
                if g < 3:
                    transposes(2 + g)

            def projection(j, par):
                for c in range(4):
                    what, half = c // 2, c % 2
                    if c == 0:
                        pe.wait_ge(wq_ready, j + 1)
                    if what:
                        pe.wait_ge(q_ready, 2 * j + half + 1)
                    elif has(j, 1, PAIRS):
                        pe.wait_ge(k_ready, 2 * j + half - 1)
                    tok = slice(half * HALF, (half + 1) * HALF)
                    terms = [(k, a, b) for k in range(KD) for a, b in
                             ((wqk_hi[par], xn_hi), (wqk_hi[par], xn_lo), (wqk_lo[par], xn_hi))]
                    for m, (k, a, b) in enumerate(terms):
                        w = slice(k * 256 + what * 128, k * 256 + what * 128 + 128)
                        last = mm(J_BANK[half][:, 0:HALF], a[:, w], b[:, k, tok],
                                  start=(m == 0), stop=(m == len(terms) - 1))
                        if m == len(terms) - 1:
                            last.then_inc(proj_done, 1)
                        yield

            pe.wait_ge(xn_ready, NT)
            passes = values(NG - 2)
            for n, _ in enumerate(projection(0, 0)):
                if n % 2:
                    next(passes, None)

            def scores(j, par, g):
                t, n = GROUPS[g]
                if g in (0, 2):
                    pe.wait_ge(k_ready, 2 * j + (1 if g == 0 else 2))
                for h in range(2):
                    if g >= 1 or has(j, 1, PAIRS):
                        read = count(pe, 12 * j + 2 * g + h - 1)
                        if g == NG - 1:
                            pe.wait_ge(ld_cols, 16)
                        pe.wait_ge(sm_ready, read)
                    elif h == 0:
                        pe.wait_ge(v_ready, 2 * NG - 2)
                    d = slice(64 * h, 64 * h + 64)
                    mm(S_BANK[h][0:n, 0:n], QT[par][d, t:t + n], KT[par][d, t:t + n],
                       start=True, stop=True).then_inc(s_done, 1)

            def probs_transposed(j, par, g):
                t, n = GROUPS[g]
                divided = count(pe, 3 * j + (1, 1, 1, 2, 2, 3)[g])
                read = count(pe, 3 * j + g // 2 + 1)
                pe.wait_ge(consts_ready, 2)
                if g in (0, 3, 5):
                    pe.wait_ge(p_ready, divided)
                if g >= 2 or has(j, 1, PAIRS):
                    pe.wait_ge(pt_ready[g % 2], read)
                for h in range(2):
                    last = nc.tensor.transpose(T_BANK[g % 2][0:n, h * UW:h * UW + n], P[par][0:n, 2 * g + h, 0:n],
                                               ident[0:n, 0:n])
                last.then_inc(t_done, 1)

            def attend(j, par, g):
                t, n = GROUPS[g]
                half, at = g // 3, t - ZHALF[g // 3][0]
                if g == 0:
                    pe.wait_ge(vp_ready, 16 * (j + 1))
                if g % 3 == 0 and has(j, 1, PAIRS):
                    pe.wait_ge(z_ready[half], j + 1)
                here = count(pe, 3 * j + g // 2 + 2)
                if g == NG - 1:
                    pe.wait_ge(ld_cols, 16)
                pe.wait_ge(pt_ready[g % 2], here)
                for h in range(2):
                    last = mm(Z_BANK[half][64 * h:64 * h + 64, at:at + n], Vp[par][0:n, g, 64 * h:64 * h + 64],
                              PT[g % 2][0:n, h, 0:n], start=True, stop=True)
                if g % 3 == 2:
                    last.then_inc(z_done[half], 1)

            def output(i, pairs):
                t, n = TILES[i]
                for j in pairs:
                    if j == 0:
                        pe.wait_ge(wo_ready, 1)
                        if i < 2:
                            pe.wait_ge(k_ready, 2 * PAIRS - 1 + i)
                        if i == 2:
                            pe.wait_ge(sm_ready, UNITS * PAIRS)
                        if i == 4:
                            pe.wait_ge(pt_ready[0], 3 * PAIRS + 1)
                    pe.wait_ge(z_ready[0], j + 2)
                    if t + n > ZHALF[0][1]:
                        pe.wait_ge(z_ready[1], j + 2)
                    tok, w = slice(j * TOKENS + t, j * TOKENS + t + n), slice(j * DIM, (j + 1) * DIM)
                    for m, (a, b) in enumerate(((z_hi, wo_hi), (z_hi, wo_lo), (z_lo, wo_hi))):
                        last = mm(O_BANK[i][0:n, 0:DIM], a[:, tok], b[:, w],
                                  start=(j == 0 and m == 0), stop=(j == PAIRS - 1 and m == 2))
                        if j == PAIRS - 1 and m == 2:
                            last.then_inc(o_done, 1)
                        yield

            def step(j, par):
                last_values = values(NG - 1) if first_step(j) else iter(())
                if has(j, 0, PAIRS - 1):
                    passes = projection(j + 1, 1 - par)
                elif j == PAIRS - 1:
                    passes = (p for i in range(2) for p in output(i, range(PAIRS - 3)))
                else:
                    passes = (p for i, pairs in ((2, range(PAIRS - 2)), (0, range(PAIRS - 3, PAIRS - 1)),
                                                 (1, range(PAIRS - 3, PAIRS - 1)), (2, range(PAIRS - 2, PAIRS - 1)),
                                                 (0, range(PAIRS - 1, PAIRS)), (1, range(PAIRS - 1, PAIRS)))
                              for p in output(i, pairs))
                for g in range(NG + 1):
                    for _ in range(PASSES_AT[g][0]):
                        next(passes, None)
                    if g < NG and has(j, 1, PAIRS + 1):
                        probs_transposed(j - 1, 1 - par, g)
                    if not has(j, 0, PAIRS):
                        next(passes, None)
                    if g >= 1 and has(j, 1, PAIRS + 1):
                        attend(j - 1, 1 - par, g - 1)
                    for _ in range(VALUES_BEFORE):
                        next(last_values, None)
                    if g < NG and has(j, 0, PAIRS):
                        scores(j, par, g)
                    for _ in range(6 - VALUES_BEFORE):
                        next(last_values, None)
                    for _ in range(PASSES_AT[g][1]):
                        next(passes, None)
                if not has(j, 0, PAIRS - 1):
                    finish(passes)
                if first_step(j):
                    pe.wait_ge(v_ready, 2 * NG)
                    pe.wait_ge(gam_done, 1)

            steps(pe, step)

            def up(c, f):
                t0, t1, _, i1 = FFN_CHUNKS[c]
                n = c * FT + f
                if f == 0:
                    pe.wait_ge(xn_ready, NT + i1)
                if n >= 3:
                    pe.wait_ge(relu_done, n - 2)
                terms = [(k, b) for k in range(KD) for b in (xn_hi, xn_lo)]
                for m, (k, b) in enumerate(terms):
                    last = mm(U_BANK[n % 3][:, 0:t1 - t0], w1q[:, k * FF + f * 128:k * FF + f * 128 + 128], b[:, k, t0:t1],
                              start=(m == 0), stop=(m == len(terms) - 1))
                last.then_inc(f1_done, 1)

            def down(i):
                t, n = TILES[i]
                chunk = 0 if i < FFN_CHUNKS[0][3] else 1
                if i < 3:
                    pe.wait_ge(h_ready, NT + 3 + i)
                for f in range(FT):
                    pe.wait_ge(ff_ready[chunk], f + 1)
                    for m, a in enumerate((h_hi, h_lo)):
                        last = mm(D_BANK[i][0:n, 0:DIM], a[:, f, t:t + n], w2q[:, f * DIM:(f + 1) * DIM],
                                  start=(f == 0 and m == 0), stop=(f == FT - 1 and m == 1))
                        if f == FT - 1 and m == 1:
                            last.then_inc(f2_done, 1)
                        yield

            finish(output(3, range(0, 4)))
            finish(output(2, range(PAIRS - 1, PAIRS)))
            finish(output(3, range(4, PAIRS)))
            pe.wait_ge(pt_ready[1], 3 * PAIRS + 1)
            finish(output(4, range(0, 2)))
            transposes(NT)
            finish(output(4, range(2, 4)))
            transposes(NT + 1)
            finish(output(4, range(4, PAIRS)))
            pe.wait_ge(wff_ready, 2)
            downs = (p for i in range(NT) for p in down(i))
            for c in range(2):
                for f in range(FT):
                    up(c, f)
                    if c == 0 and f in TILE_AFTER:
                        transposes(NT + TILE_AFTER[f])
                    for _ in range(DOWNS_AT[c][f]):
                        next(downs, None)
            finish(downs)


def kernel(**inputs):
    import numpy as np
    import concourse.bacc as bacc
    from concourse.bass_utils import run_bass_kernel_spmd

    def two(a, width):
        return np.ascontiguousarray(a.reshape(-1, 128, width).transpose(1, 0, 2))

    g = {k: np.asarray(v) for k, v in inputs.items()}
    p = g["x"].reshape(IMAGES, 3, 6, 16, 6, 16).transpose(0, 2, 4, 1, 3, 5).reshape(IMAGES, SEQ - 1, PATCH_DIM)
    tok = np.zeros((IMAGES, SEQ, PATCH_DIM), p.dtype)
    tok[:, 1:] = p
    xt = tok.reshape(TOKENS, PATCH_DIM).T.reshape(KP, 128, TOKENS)
    wt = g["L0_tok_W"].T.reshape(KP, 128, DIM)
    wq, wk, wvt = (g[f"L0_attn_W_{n}"].reshape(HEADS * HEAD_DIM, DIM).T for n in "QKV")
    wqk = np.stack([a.reshape(KD, 128, PAIRS, 128) for a in (wq, wk)], 3)
    arrays = {
        "xw": np.ascontiguousarray(np.concatenate([xt, wt], 2)),
        "wqk": np.ascontiguousarray(wqk.transpose(1, 2, 0, 3, 4)).reshape(128, PAIRS * KD * 256),
        "wv": two(wvt, FF),
        "wo": two(g["L0_attn_W_O"].transpose(0, 2, 1).reshape(HEADS * HEAD_DIM, DIM), DIM).reshape(128, PAIRS * DIM),
        "w1": two(g["L0_ffn_W1"].T, FF).reshape(128, KD * FF),
        "w2": two(g["L0_ffn_W2"].T, DIM).reshape(128, FT * DIM),
        "bias_cols": np.ascontiguousarray(np.concatenate(
            [g[n].reshape(8, 128).T for n in ("L0_attn_b_Q", "L0_attn_b_K", "L0_attn_b_V", "L0_ffn_b1")], 1)),
        "bias_rows": np.concatenate([g["L0_attn_b_O"], g["L0_ffn_b2"]]).reshape(1, 2 * DIM),
        "tok_bias": g["L0_tok_b"].reshape(1, DIM),
        "cls": g["L0_tok_cls_token"].reshape(1, DIM),
        "pos": np.ascontiguousarray(g["L0_tok_pos_embed"].reshape(SEQ, DIM)),
    }
    nc = bacc.Bacc("TRN2", target_bir_lowering=False, num_devices=1)
    args = [nc.dram_tensor(f"in_{n}", a.shape, mybir.dt.from_np(a.dtype), kind="ExternalInput").ap()
            for n, a in arrays.items()]
    out = nc.dram_tensor("out", (TOKENS, DIM), F32, kind="ExternalOutput").ap()
    vit_block(nc, *args, out)
    r = run_bass_kernel_spmd(nc, [{f"in_{n}": a for n, a in arrays.items()}], core_ids=[0])
    return r.results[0]["out"].reshape(IMAGES, SEQ, DIM)
```
